# Optimizing a Trainium2 kernel written in Bass

```python
import numpy as np
import jax
import jax.numpy as jnp

def _softmax(x, axis=-1):
    return jax.nn.softmax(x, axis=axis)

def _gelu(x):
    return jax.nn.gelu(x, approximate=True)

def _silu(x):
    return jax.nn.silu(x)

def _sigmoid(x):
    return jax.nn.sigmoid(x)

def _layernorm(x, axis=-1, eps=1e-05):
    m = jnp.mean(x, axis=axis, keepdims=True)
    v = jnp.var(x, axis=axis, keepdims=True)
    return (x - m) / jnp.sqrt(v + eps)

def _scatter_add(tgt, idx, src, axis=0):
    return tgt.at[idx].add(src)

def _segment_sum(src, seg, n):
    return jax.ops.segment_sum(src, seg, n)
kernel_name = 'mk_adj_resnorm_d1_adj_r2_ab6410'

def setup_inputs(seed: int=0):
    np.random.seed(seed)
    _w = jnp.asarray

    def _rec_inputs():
        import jax
        import jax.numpy as jnp
        _gk = jax.random.key(seed)
        x = 7.22e-05 + 1 * jax.random.normal(jax.random.fold_in(_gk, 1), (8, 2048, 128), jnp.float32)
        _a = jax.random.bernoulli(jax.random.fold_in(_gk, 2), 0.0078125, (2048, 2048))
        _a = jnp.logical_or(_a, jnp.swapaxes(_a, -1, -2))
        _a = jnp.logical_or(_a, jnp.eye(2048, dtype=bool))
        _af = _a.astype(jnp.float32)
        _af = _af * jax.random.uniform(jax.random.fold_in(_gk, 3), (2048, 2048), jnp.float32, 0.05, 0.119748)
        adj = _af
        return (x, adj)
    x, adj = _rec_inputs()

    def _L0_gnn_setup():
        import jax, jax.numpy as jnp
        import numpy as np
        B, N, F_IN, F_OUT = (8, 2048, 128, 128)
        key = jax.random.key(seed)
        k1, k2, k3 = jax.random.split(key, 3)
        H = jax.random.normal(k1, (B, N, F_IN), dtype=jnp.float32)
        W = jax.random.normal(k2, (F_IN, F_OUT), dtype=jnp.float32) * (1.0 / np.sqrt(F_IN))
        A = jax.random.normal(k3, (N, N), dtype=jnp.float32) * (1.414 * np.sqrt(2.0 / (N + N)))
        return {'H': H, 'W': W, 'A': A}
    _L0_gnn_all = _L0_gnn_setup()
    _L0_gnn_in = {k: v for k, v in _L0_gnn_all.items() if k in ('W',)}
    del _L0_gnn_all
    return {'x': x, 'adj': adj, 'L0_gnn_W': _L0_gnn_in['W']}

def reference(x, adj, L0_gnn_W):
    import jax
    import jax.numpy as jnp

    def _L0_gnn_ref(H, W, A):
        import jax, jax.numpy as jnp
        import numpy as np
        B, N, F_IN, F_OUT = (8, 2048, 128, 128)
        HW = jnp.einsum('bnf,fo->bno', H, W)
        A_norm = jax.nn.relu((A + A.T) * 0.5)
        D = jnp.sum(A_norm, axis=1)
        D_safe = jnp.where(D > 0, D, 1.0)
        d_inv_sqrt = jnp.where(D > 0, D_safe ** (-0.5), 0.0)
        DAD = d_inv_sqrt[:, None] * A_norm * d_inv_sqrt[None, :]
        L_norm = jnp.eye(N, dtype=H.dtype) - DAD
        out = jnp.einsum('nm,bmo->bno', L_norm, HW)
        return jax.nn.relu(out)
    x = _layernorm(x + _L0_gnn_ref(x, L0_gnn_W, adj), axis=-1)
    return x

_drawn_inputs = setup_inputs


def setup_inputs(seed=0):
    import zlib

    import numpy as np

    out = dict(_drawn_inputs(seed))
    spreads = {}
    factors = {}
    for name, (base, spread) in spreads.items():
        noise = np.random.default_rng([zlib.crc32(name.encode()), seed]).standard_normal(out[name].shape)
        drawn = base * np.exp(spread * noise) if base else spread * noise
        out[name] = jnp.asarray(drawn.astype(out[name].dtype))
    for name, factor in factors.items():
        out[name] = (out[name] * factor).astype(out[name].dtype)
    return out
```

```python
from contextlib import ExitStack

import concourse.bass as bass
from concourse import mybir

B, N, F = 8, 2048, 128
P = 128
TILES = N // P
HALF_B = B // 2
HALF = HALF_B * F
HALVES = 2 * TILES
EPS = 1e-5
L_SCALE = 2.0 ** 15
HW_TOP = 2.0 ** 13
QUARTER = TILES // 4
SPLIT_EARLY = 16


def triangle():
    return [(i, j0, min(4, i + 1 - j0)) for i in range(TILES) for j0 in range(0, i + 1, 4)]


def gcn_layernorm(nc, x, adj, w, out):
    f32, f16, i32 = mybir.dt.float32, mybir.dt.float16, mybir.dt.int32
    ALU, ACT, AX = mybir.AluOpType, mybir.ActivationFunctionType, mybir.AxisListType

    x_tiles = x.rearrange("b (t p) f -> t p b f", p=P)
    out_tiles = out.rearrange("b (t p) f -> t p b f", p=P)
    adj_tiles = adj.rearrange("(t p) n -> t p n", p=P)

    GROUPS = triangle()
    MIRRORED = [k for k, (i, j0, nb) in enumerate(GROUPS) if j0 < i]

    ctx = ExitStack()
    with ctx:
        def sb(name, shape, dt):
            return ctx.enter_context(nc.sbuf_tensor(name, shape, dt))

        def sem(name):
            return ctx.enter_context(nc.semaphore(name))

        S = sb("S", [P, TILES, N], f32)
        H = sb("H", [P, HALVES + 2, HALF], f32)
        Hs = H[:, :, :].bitcast(f16)
        Lh = sb("Lh", [P, TILES, P], f16)
        Ll = sb("Ll", [P, TILES, P], f16)
        ident = sb("ident", [P, P], f32)
        ones = sb("ones", [P, P], f32)
        w_sb = sb("w_sb", [P, F], f32)
        diag = sb("diag", [P, 4, P], f32)
        peak = sb("peak", [P, HALVES], f32)
        peak1 = sb("peak1", [P, 1], f32)
        peakrow = sb("peakrow", [1, P], f32)
        peakall = sb("peakall", [1, 1], f32)
        power = sb("power", [P, 1], f32)
        inverse = sb("inverse", [P, 1], f32)
        hw_scale = sb("hw_scale", [P, 1], f32)
        unscale = sb("unscale", [P, 1], f32)
        rowpart = sb("rowpart", [P, TILES, 4], f32)
        dlow = sb("dlow", [P, TILES], f32)
        dhigh = sb("dhigh", [P, TILES], f32)
        deg = sb("deg", [P, TILES], f32)
        degs = sb("degs", [P, TILES], f32)
        droot = sb("droot", [P, TILES], f32)
        dinv = sb("dinv", [P, TILES], f32)
        dtmp = sb("dtmp", [P, TILES], f32)
        dneg = sb("dneg", [P, TILES], f32)
        conv = sb("conv", [P, B * F], f32)
        stats = sb("stats", [P, B, 6], f32)
        mv = sb("mv", [P, B, 2], f32)
        var = sb("var", [P, B], f32)
        std = sb("std", [P, B], f32)
        rstd = sb("rstd", [P, B], f32)
        ntmp = sb("ntmp", [P, B], f32)
        epsc = sb("epsc", [P, 1], f32)

        bank = [ctx.enter_context(nc.psum_tensor(f"bank{n}", [P, HALF], f32)) for n in range(8)]
        turned = bank[0:4]
        second = bank[4:6]
        colsum = bank[6][:, 0:TILES * TILES].rearrange("p (j i) -> p j i", i=TILES)
        misc = bank[7]
        product = bank[0:4]
        drow = bank[4:8]

        def x_stage(t):
            return S[:, 7 + t // 2, (t % 2) * B * F:(t % 2 + 1) * B * F].rearrange("p (b f) -> p b f", b=B)

        def xT_stage(k):
            return S[:, TILES - 1, (k % 4) * HALF:(k % 4 + 1) * HALF]

        def columns(t):
            return S[:, :, bass.ds(t * P, P)]

        w_loaded = sem("w_loaded")
        x_loaded = [sem(f"x_loaded{t}") for t in range(TILES)]
        adj_loaded = [sem(f"adj_loaded{i}") for i in range(TILES)]
        consts = sem("consts")
        x_turned = sem("x_turned")
        xT_copied = sem("xT_copied")
        hw_done = sem("hw_done")
        hw_kept = sem("hw_kept")
        peak_kept = sem("peak_kept")
        peak_step = sem("peak_step")
        peak_turned = sem("peak_turned")
        peak_spread = sem("peak_spread")
        scale_ready = sem("scale_ready")
        hw_high = sem("hw_high")
        hw_low = sem("hw_low")
        adj_turned = sem("adj_turned")
        sums_done = sem("sums_done")
        relu_done = sem("relu_done")
        s_turned = sem("s_turned")
        mirrored_dve = sem("mirrored_dve")
        mirrored_act = sem("mirrored_act")
        deg_step = sem("deg_step")
        deg_ready = sem("deg_ready")
        root_done = sem("root_done")
        diag_ready = sem("diag_ready")
        drow_ready = sem("drow_ready")
        l_step = sem("l_step")
        l_ready = sem("l_ready")
        l_high = sem("l_high")
        l_low = sem("l_low")
        quarter_used = sem("quarter_used")
        conv_used = sem("conv_used")
        relu_out = sem("relu_out")
        res_loaded = [sem("res_loaded_even"), sem("res_loaded_odd")]
        n_step = sem("n_step")
        var_ready = sem("var_ready")
        std_ready = sem("std_ready")
        out_ready = sem("out_ready")
        stored = sem("stored")

        def early(k):
            return MIRRORED.index(k) % 3 != 2

        def copied_before(k, by_dve):
            return sum(early(m) == by_dve for m in MIRRORED if m < k)

        block = ctx.enter_context(nc.Block())

        @block.sync
        def _(sp):
            sp.dma_start(x_stage(0), x_tiles[0]).then_inc(x_loaded[0], 16)
            sp.dma_start(w_sb[:, :], w).then_inc(w_loaded, 16)
            for t in range(1, TILES):
                sp.dma_start(x_stage(t), x_tiles[t]).then_inc(x_loaded[t], 16)
            for i in range(TILES):
                if i == TILES - 1:
                    sp.wait_ge(hw_done, HALVES)
                elif i >= 7:
                    sp.wait_ge(x_turned, 4 * (i - 6))
                sp.dma_start(S[:, i, :], adj_tiles[i]).then_inc(adj_loaded[i], 16)

            def residual(t, parity):
                sp.wait_ge(l_high, 4 * t + 4)
                sp.wait_ge(l_low, 4 * t + 4)
                sp.dma_start(columns(t)[:, 0:B, :], x_tiles[bass.ds(t, 1)].rearrange("t p b f -> (t p) b f"))\
                  .then_inc(res_loaded[parity], 16)

            def store(t):
                sp.wait_ge(out_ready, t + 1)
                sp.dma_start(out_tiles[bass.ds(t, 1)].rearrange("t p b f -> (t p) b f"), columns(t)[:, B:2 * B, :])\
                  .then_inc(stored, 16)

            residual(0, 0)
            residual(1, 1)
            store(0)
            with sp.Fori(1, TILES - 2, 2) as t:
                residual(t + 1, 0)
                store(t)
                residual(t + 2, 1)
                store(t + 1)
            store(TILES - 1)
            sp.wait_ge(stored, 16 * TILES)

        @block.gpsimd
        def _(pool):
            nc.gpsimd.memset(ident[:, :], 0.0).then_inc(consts, 1)
            nc.gpsimd.memset(ones[:, :], 1.0).then_inc(consts, 1)
            nc.gpsimd.memset(rowpart[:, :, :], 0.0).then_inc(consts, 1)
            nc.gpsimd.memset(epsc[:, :], EPS).then_inc(consts, 1)
            pool.wait_ge(consts, 4)
            nc.gpsimd.affine_select(out=ident[:, :], in_=ident[:, :], compare_op=ALU.not_equal, fill=1.0,
                                    base=0, pattern=[[-1, P]], channel_multiplier=1).then_inc(consts, 1)

        @block.tensor
        def _(pe):
            pe.wait_ge(consts, 5)
            pe.wait_ge(w_loaded, 16)

            def turn_x(k):
                t, half = divmod(k, 2)
                pe.wait_ge(x_loaded[t], 16)
                if k >= 4:
                    pe.wait_ge(xT_copied, k - 3)
                for b in range(HALF_B):
                    last = nc.tensor.transpose(turned[k % 4][:, b * P:(b + 1) * P],
                                               x_stage(t)[:, half * HALF_B + b, :], ident[:, :])
                last.then_inc(x_turned, 1)

            def times_w(k):
                pe.wait_ge(xT_copied, k + 1)
                if k >= 2:
                    pe.wait_ge(peak_kept, k - 1)
                for b in range(HALF_B):
                    last = nc.tensor.matmul(second[k % 2][:, b * F:(b + 1) * F], xT_stage(k)[:, b * P:(b + 1) * P],
                                            w_sb[:, :], start=True, stop=True)
                last.then_inc(hw_done, 1)

            for k in range(HALVES + 2):
                if k < HALVES:
                    turn_x(k)
                if k >= 2:
                    times_w(k - 2)

            pe.wait_ge(peak_step, 1)
            nc.tensor.transpose(misc[0:1, 0:P], peak1[:, :], ident[:, :]).then_inc(peak_turned, 1)
            pe.wait_ge(peak_step, 2)
            nc.tensor.matmul(misc[:, P:P + 1], ones[0:1, :], peakall[:, :], start=True, stop=True)\
              .then_inc(peak_spread, 1)

            def turn_adj(k):
                i, j0, nb = GROUPS[k]
                pe.wait_ge(adj_loaded[j0 + nb - 1], 16)
                if k >= 4:
                    pe.wait_ge(sums_done, k - 3)
                else:
                    pe.wait_ge(xT_copied, HALVES - 3 + k)
                for n in range(nb):
                    last = nc.tensor.transpose(turned[k % 4][:, n * P:(n + 1) * P],
                                               S[:, j0 + n, i * P:(i + 1) * P], ident[:, :])
                last.then_inc(adj_turned, 1)

            def turn_s(k):
                m = MIRRORED.index(k)
                i, j0, nb = GROUPS[k]
                pe.wait_ge(relu_done, k + 1)
                if m >= 2:
                    b4 = MIRRORED[m - 2]
                    pe.wait_ge(mirrored_dve if early(b4) else mirrored_act, copied_before(b4, early(b4)) + 1)
                else:
                    pe.wait_ge(peak_kept, HALVES)
                for n in range(min(nb, i - j0)):
                    block_ij = S[:, i, (j0 + n) * P:(j0 + n + 1) * P]
                    nc.tensor.transpose(second[m % 2][:, n * P:(n + 1) * P], block_ij, ident[:, :])
                    last = nc.tensor.matmul(colsum[:, j0 + n, i:i + 1], block_ij, ones[:, 0:1],
                                            start=True, stop=True)
                last.then_inc(s_turned, 1)

            pe.wait_ge(peak_step, 3)
            for k in range(len(GROUPS) + 2):
                if k < len(GROUPS):
                    turn_adj(k)
                if k - 2 in MIRRORED:
                    turn_s(k - 2)

            def spread_d(q):
                pe.wait_ge(diag_ready, q + 1)
                nc.tensor.matmul(drow[q][:, :], ones[:, :], diag[:, :, :].rearrange("p t n -> p (t n)"),
                                 start=True, stop=True).then_inc(drow_ready, 1)

            for q in range(4):
                spread_d(q)

            def quarter(t, parity, q, first):
                pe.wait_ge(l_low, 4 * t + q + 1)
                if first:
                    pe.wait_ge(hw_low, 2 * QUARTER * (q + 1))
                for m in range(q * QUARTER, (q + 1) * QUARTER):
                    for left, part in ((Lh, 0), (Lh, 1), (Ll, 0)):
                        for half in range(2):
                            right = Hs[:, 2 * m + half, part * HALF:(part + 1) * HALF]
                            last = nc.tensor.matmul(product[2 * parity + half][:, :], left[:, m, :], right,
                                                    start=(m == 0 and left is Lh and part == 0),
                                                    stop=(m == TILES - 1 and left is Ll))
                last.then_inc(quarter_used, 1)

            def tile(t, parity, first=False, reuse=True):
                if reuse:
                    pe.wait_ge(relu_out, 2 * t - 2)
                for q in range(4):
                    quarter(t, parity, q, first)

            tile(0, 0, first=True, reuse=False)
            tile(1, 1, reuse=False)
            with pe.Fori(2, TILES - 1, 2) as t:
                tile(t, 0)
                tile(t + 1, 1)

        @block.scalar
        def _(act):
            for k in range(HALVES):
                act.wait_ge(x_turned, k + 1)
                if k >= 4:
                    act.wait_ge(hw_done, k - 3)
                nc.scalar.activation(xT_stage(k), turned[k % 4][:, :], ACT.Copy).then_inc(xT_copied, 1)

            def high(k):
                if k >= 2:
                    act.wait_ge(hw_low, k - 1)
                nc.scalar.activation(Hs[:, k, 0:HALF], H[:, k + 2, :], ACT.Copy, scale=hw_scale[:, :])\
                  .then_inc(hw_high, 1)

            def relu(k):
                i, j0, nb = GROUPS[k]
                area = S[:, i, j0 * P:(j0 + nb) * P]
                act.wait_ge(sums_done, k + 1)
                nc.scalar.activation(area, area, ACT.Relu, scale=0.5, accum_out=rowpart[:, i, j0 // 4:j0 // 4 + 1])\
                  .then_inc(relu_done, 1)

            def mirror(k):
                i, j0, nb = GROUPS[k]
                m, nb = MIRRORED.index(k), min(nb, i - j0)
                act.wait_ge(s_turned, m + 1)
                nc.scalar.activation(S[:, j0:j0 + nb, i * P:(i + 1) * P],
                                     second[m % 2][:, 0:nb * P].rearrange("p (t n) -> p t n", n=P), ACT.Copy)\
                  .then_inc(mirrored_act, 1)

            act.wait_ge(consts, 5)
            split = 0
            for k in range(len(GROUPS) + 3):
                if k < len(GROUPS):
                    relu(k)
                if k - 3 in MIRRORED and not early(k - 3):
                    mirror(k - 3)
                if k == 3:
                    act.wait_ge(scale_ready, 1)
                if k >= 3 and k % 2 and split < SPLIT_EARLY:
                    high(split)
                    split += 1

            act.wait_ge(deg_ready, 1)
            nc.scalar.activation(droot[:, :], degs[:, :], ACT.Sqrt).then_inc(root_done, 1)

            def l_highs(t, first=False):
                act.wait_ge(l_ready, t + 1)
                for q in range(4):
                    if not first:
                        act.wait_ge(quarter_used, 4 * t + q - 3)
                    nc.scalar.activation(Lh[:, q * QUARTER:(q + 1) * QUARTER, :],
                                         columns(t)[:, q * QUARTER:(q + 1) * QUARTER, :], ACT.Copy)\
                      .then_inc(l_high, 1)

            def norm(t, parity, reuse=True):
                if reuse:
                    act.wait_ge(conv_used, t)
                act.wait_ge(peak_step, 7)
                act.wait_ge(quarter_used, 4 * t + 4)
                for half in range(2):
                    nc.scalar.activation(conv[:, half * HALF:(half + 1) * HALF], product[2 * parity + half][:, :],
                                         ACT.Relu, scale=unscale[:, :]).then_inc(relu_out, 1)
                act.wait_ge(var_ready, t + 1)
                nc.scalar.activation(std[:, :], var[:, :], ACT.Sqrt).then_inc(std_ready, 1)

            l_highs(0, first=True)
            for k in range(split, HALVES):
                high(k)
            l_highs(1)
            norm(0, 0, reuse=False)
            with act.Fori(1, TILES - 2, 2) as t:
                l_highs(t + 1)
                norm(t, 1)
                l_highs(t + 2)
                norm(t + 1, 0)
            norm(TILES - 1, 1)

        @block.vector
        def _(dve):
            for k in range(HALVES):
                dve.wait_ge(hw_done, k + 1)
                nc.vector.tensor_copy(H[:, k + 2, :], second[k % 2][:, :]).then_inc(hw_kept, 1)
                nc.vector.tensor_reduce(peak[:, k:k + 1], second[k % 2][:, :], AX.X, ALU.max,
                                        apply_absolute_value=True).then_inc(peak_kept, 1)
            dve.wait_ge(peak_kept, HALVES)
            nc.vector.tensor_reduce(peak1[:, :], peak[:, :], AX.X, ALU.max).then_inc(peak_step, 1)
            dve.wait_ge(peak_turned, 1)
            nc.vector.tensor_reduce(peakall[:, :], misc[0:1, 0:P], AX.X, ALU.max).then_inc(peak_step, 1)
            nc.vector.memset(bank[6][:, :], 0.0).then_inc(peak_step, 1)
            dve.wait_ge(peak_spread, 1)
            nc.vector.tensor_scalar(power[:, :], misc[:, P:P + 1], 2.0 ** -100, 2.0 ** 126, ALU.max, ALU.min)\
              .then_inc(peak_step, 1)
            dve.wait_ge(peak_step, 4)
            nc.vector.tensor_scalar(power[:, :].bitcast(i32), power[:, :].bitcast(i32), 0x7F800000, None,
                                    ALU.bitwise_and).then_inc(peak_step, 1)
            dve.wait_ge(peak_step, 5)
            nc.vector.tensor_scalar(inverse[:, :].bitcast(i32), power[:, :].bitcast(i32), -1.0,
                                    float(254 << 23), ALU.mult, ALU.add).then_inc(peak_step, 1)
            nc.vector.tensor_scalar(unscale[:, :], power[:, :], 1.0 / (HW_TOP * L_SCALE), None, ALU.mult)\
              .then_inc(peak_step, 1)
            dve.wait_ge(peak_step, 7)
            nc.vector.tensor_scalar(hw_scale[:, :], inverse[:, :], HW_TOP, None, ALU.mult).then_inc(scale_ready, 1)

            def low(k):
                dve.wait_ge(hw_high, k + 1)
                nc.vector.scalar_tensor_tensor(out=Hs[:, k, HALF:2 * HALF], in0=H[:, k + 2, :],
                                               scalar=hw_scale[:, :], in1=Hs[:, k, 0:HALF],
                                               op0=ALU.mult, op1=ALU.subtract).then_inc(hw_low, 1)

            def add(k):
                i, j0, nb = GROUPS[k]
                area = S[:, i, j0 * P:(j0 + nb) * P]
                dve.wait_ge(adj_loaded[i], 16)
                dve.wait_ge(adj_turned, k + 1)
                nc.vector.tensor_tensor(area, area, turned[k % 4][:, 0:nb * P], ALU.add).then_inc(sums_done, 1)

            def mirror(k):
                i, j0, nb = GROUPS[k]
                m, nb = MIRRORED.index(k), min(nb, i - j0)
                dve.wait_ge(s_turned, m + 1)
                nc.vector.tensor_copy(S[:, j0:j0 + nb, i * P:(i + 1) * P],
                                      second[m % 2][:, 0:nb * P].rearrange("p (t n) -> p t n", n=P))\
                  .then_inc(mirrored_dve, 1)

            split = 0
            dve.wait_ge(scale_ready, 1)
            for k in range(len(GROUPS) + 3):
                if k < len(GROUPS):
                    add(k)
                if k - 3 in MIRRORED and early(k - 3):
                    mirror(k - 3)
                if k >= 3 and k % 2 and split < SPLIT_EARLY:
                    low(split)
                    split += 1

            dve.wait_ge(relu_done, len(GROUPS))
            nc.vector.tensor_reduce(dlow[:, :], rowpart[:, :, :], AX.X, ALU.add).then_inc(deg_step, 1)
            dve.wait_ge(s_turned, len(MIRRORED))
            nc.vector.tensor_reduce(dhigh[:, :], colsum, AX.X, ALU.add).then_inc(deg_step, 1)
            dve.wait_ge(deg_step, 2)
            nc.vector.tensor_tensor(deg[:, :], dlow[:, :], dhigh[:, :], ALU.add).then_inc(deg_step, 1)
            dve.wait_ge(deg_step, 3)
            nc.vector.scalar_tensor_tensor(out=degs[:, :], in0=deg[:, :], scalar=0.0, in1=deg[:, :],
                                           op0=ALU.is_le, op1=ALU.add).then_inc(deg_ready, 1)
            dve.wait_ge(root_done, 1)
            nc.vector.reciprocal(dinv[:, :], droot[:, :]).then_inc(deg_step, 1)
            dve.wait_ge(deg_step, 4)
            nc.vector.tensor_tensor(dtmp[:, :], dinv[:, :], dinv[:, :], ALU.mult).then_inc(deg_step, 1)
            dve.wait_ge(deg_step, 5)
            nc.vector.tensor_tensor(dtmp[:, :], dtmp[:, :], degs[:, :], ALU.mult).then_inc(deg_step, 1)
            dve.wait_ge(deg_step, 6)
            nc.vector.tensor_scalar(dtmp[:, :], dtmp[:, :], -0.5, 1.5, ALU.mult, ALU.add).then_inc(deg_step, 1)
            dve.wait_ge(deg_step, 7)
            nc.vector.tensor_tensor(dinv[:, :], dinv[:, :], dtmp[:, :], ALU.mult).then_inc(deg_step, 1)
            dve.wait_ge(deg_step, 8)
            nc.vector.scalar_tensor_tensor(out=dinv[:, :], in0=deg[:, :], scalar=0.0, in1=dinv[:, :],
                                           op0=ALU.is_gt, op1=ALU.mult).then_inc(deg_step, 1)
            dve.wait_ge(deg_step, 9)
            nc.vector.tensor_scalar(dneg[:, :], dinv[:, :], -L_SCALE, None, ALU.mult).then_inc(deg_step, 1)
            dve.wait_ge(deg_step, 10)
            for q in range(4):
                if q:
                    dve.wait_ge(drow_ready, q)
                nc.vector.tensor_tensor(diag[:, :, :], ident[:, :].unsqueeze(1).to_broadcast([P, 4, P]),
                                        dneg[:, 4 * q:4 * q + 4].unsqueeze(2).to_broadcast([P, 4, P]), ALU.mult)\
                  .then_inc(diag_ready, 1)
            dve.wait_ge(drow_ready, 4)


            def l_tile(t, q, r):
                cols = columns(t)
                nc.vector.tensor_tensor(cols, cols, dinv[:, :].unsqueeze(2).to_broadcast([P, TILES, P]), ALU.mult)\
                  .then_inc(l_step, 1)
                dve.wait_ge(l_step, t * 2 + 1)
                nc.vector.tensor_tensor(cols, cols,
                                        drow[q][:, r * P:(r + 1) * P].unsqueeze(1).to_broadcast([P, TILES, P]),
                                        ALU.mult).then_inc(l_step, 1)
                dve.wait_ge(l_step, t * 2 + 2)
                dblock = S[:, bass.ds(t, 1), bass.ds(t * P, P)].rearrange("p o n -> p (o n)")
                nc.vector.scalar_tensor_tensor(out=dblock, in0=ident[:, :], scalar=L_SCALE, in1=dblock,
                                               op0=ALU.mult, op1=ALU.add).then_inc(l_ready, 1)

            def l_lows(t):
                for q in range(4):
                    dve.wait_ge(l_high, 4 * t + q + 1)
                    part = slice(q * QUARTER, (q + 1) * QUARTER)
                    nc.vector.tensor_tensor(Ll[:, part, :], columns(t)[:, part, :], Lh[:, part, :], ALU.subtract)\
                      .then_inc(l_low, 1)

            N_STEPS = 7

            def norm(t):
                cols = columns(t)
                n0 = t * N_STEPS
                dve.wait_ge(relu_out, 2 * t + 2)
                dve.wait_ge(res_loaded[t % 2], 16 * (t // 2 + 1))
                nc.vector.tensor_tensor(cols[:, B:2 * B, :], conv[:, :].rearrange("p (b f) -> p b f", f=F),
                                        cols[:, 0:B, :], ALU.add).then_inc(conv_used, 1)
                dve.wait_ge(conv_used, t + 1)
                for b in range(B):
                    last = nc.vector.bn_stats(stats[:, b, :], cols[:, B + b, :])
                last.then_inc(n_step, 1)
                dve.wait_ge(n_step, n0 + 1)
                for b in range(B):
                    last = nc.vector.bn_aggr(mv[:, b, :], stats[:, b, :])
                last.then_inc(n_step, 1)
                dve.wait_ge(n_step, n0 + 2)
                nc.vector.tensor_scalar(var[:, :], mv[:, :, 1], EPS, None, ALU.add).then_inc(var_ready, 1)
                dve.wait_ge(std_ready, t + 1)
                nc.vector.reciprocal(rstd[:, :], std[:, :]).then_inc(n_step, 1)
                dve.wait_ge(n_step, n0 + 3)
                nc.vector.tensor_tensor(ntmp[:, :], rstd[:, :], rstd[:, :], ALU.mult).then_inc(n_step, 1)
                dve.wait_ge(n_step, n0 + 4)
                nc.vector.tensor_tensor(ntmp[:, :], ntmp[:, :], var[:, :], ALU.mult).then_inc(n_step, 1)
                dve.wait_ge(n_step, n0 + 5)
                nc.vector.tensor_scalar(ntmp[:, :], ntmp[:, :], -0.5, 1.5, ALU.mult, ALU.add).then_inc(n_step, 1)
                dve.wait_ge(n_step, n0 + 6)
                nc.vector.tensor_tensor(rstd[:, :], rstd[:, :], ntmp[:, :], ALU.mult).then_inc(n_step, 1)
                dve.wait_ge(n_step, n0 + 7)
                for b in range(B):
                    last = nc.vector.tensor_scalar(cols[:, B + b, :], cols[:, B + b, :], mv[:, b, 0:1],
                                                   rstd[:, b:b + 1], ALU.subtract, ALU.mult)
                last.then_inc(out_ready, 1)

            l_tile(0, 0, 0)
            l_lows(0)
            for k in range(split, HALVES):
                low(k)
            for r in range(1, 4):
                l_tile(r, 0, r)
                l_lows(r)
                norm(r - 1)
            for q in range(1, 4):
                for r in range(4):
                    l_tile(4 * q + r, q, r)
                    l_lows(4 * q + r)
                    norm(4 * q + r - 1)
            norm(TILES - 1)


def kernel(x, adj, L0_gnn_W):
    import numpy as np
    import concourse.bacc as bacc
    from concourse.bass_utils import run_bass_kernel_spmd

    nc = bacc.Bacc("TRN2", target_bir_lowering=False, num_devices=1, dynamic_dma_scratch_size=1024)
    arrays, args = {}, []
    for name, a in (("x", x), ("adj", adj), ("L0_gnn_W", L0_gnn_W)):
        a = np.ascontiguousarray(a)
        arrays[f"in_{name}"] = a
        args.append(nc.dram_tensor(f"in_{name}", a.shape, mybir.dt.from_np(a.dtype), kind="ExternalInput").ap())
    args.append(nc.dram_tensor("out", (B, N, F), mybir.dt.float32, kind="ExternalOutput").ap())
    gcn_layernorm(nc, *args)
    return run_bass_kernel_spmd(nc, [arrays], core_ids=[0]).results[0]["out"]
```

```python
from contextlib import ExitStack

import concourse.bass as bass
from concourse import mybir

B, N, F = 8, 2048, 128
P = 128
TILES = N // P
HALF_B = B // 2
HALF = HALF_B * F
HALVES = 2 * TILES
EPS = 1e-5
L_SCALE = 2.0 ** 15
HW_TOP = 2.0 ** 13
LEAD = 4
LAG = 3
QUARTER = TILES // 4
SECOND = 3
SPLIT_EARLY = 8


def triangle():
    return [(i, j0, min(4, i + 1 - j0)) for i in range(TILES) for j0 in range(0, i + 1, 4)]


def arrivals():
    order = [("x", t) for t in range(LEAD)]
    for i in range(TILES):
        order.append(("adj", i))
        if LEAD + i < TILES:
            order.append(("x", LEAD + i))
    return order


def steps():
    order = [("x", k) for k in range(2 * LEAD)]
    groups = triangle()
    for i in range(TILES):
        ours = [("adj", k) for k, g in enumerate(groups) if g[0] == i]
        halves = [("x", k) for k in range(2 * (LEAD + i), min(2 * (LEAD + i) + 2, HALVES))]
        while ours or halves:
            order += ours[:1] + halves[:1]
            ours, halves = ours[1:], halves[1:]
    return order


def gcn_layernorm(nc, x, adj, w, out):
    f32, f16, i32 = mybir.dt.float32, mybir.dt.float16, mybir.dt.int32
    ALU, ACT, AX = mybir.AluOpType, mybir.ActivationFunctionType, mybir.AxisListType

    x_tiles = x.rearrange("b (t p) f -> t p b f", p=P)
    out_tiles = out.rearrange("b (t p) f -> t p b f", p=P)
    adj_tiles = adj.rearrange("(t p) n -> t p n", p=P)

    GROUPS = triangle()
    MIRRORED = [k for k, (i, j0, nb) in enumerate(GROUPS) if j0 < i]

    STEPS = steps()
    X_END = max(n for n, (kind, _) in enumerate(STEPS) if kind == "x") + LAG + 3
    SECONDS = [n for n, (kind, k) in enumerate(STEPS) if kind == "x" or k in MIRRORED]

    ctx = ExitStack()
    with ctx:
        def sb(name, shape, dt):
            return ctx.enter_context(nc.sbuf_tensor(name, shape, dt))

        def sem(name):
            return ctx.enter_context(nc.semaphore(name))

        S = sb("S", [P, TILES, N], f32)
        H = sb("H", [P, HALVES + 2, HALF], f32)
        Hs = H[:, :, :].bitcast(f16)
        L16 = sb("L16", [P, 2, TILES, P], f16)
        Lh, Ll = L16[:, 0], L16[:, 1]
        above = L16[:, :, :, :].rearrange("p a t n -> p (a t n)").bitcast(f32)\
                               .rearrange("p (t n) -> p t n", n=P)
        ident = sb("ident", [P, P], f32)
        ones = sb("ones", [P, P], f32)
        w_sb = sb("w_sb", [P, F], f32)
        diag = sb("diag", [P, 4 * P], f32)
        peak = sb("peak", [P, HALVES], f32)
        peak1 = sb("peak1", [P, 1], f32)
        peakrow = sb("peakrow", [1, P], f32)
        peakall = sb("peakall", [1, 1], f32)
        power = sb("power", [P, 1], f32)
        inverse = sb("inverse", [P, 1], f32)
        hw_scale = sb("hw_scale", [P, 1], f32)
        unscale = sb("unscale", [P, 1], f32)
        rowpart = sb("rowpart", [P, TILES, 4], f32)
        dlow = sb("dlow", [P, TILES], f32)
        dhigh = sb("dhigh", [P, TILES], f32)
        deg = sb("deg", [P, TILES], f32)
        degs = sb("degs", [P, TILES], f32)
        droot = sb("droot", [P, TILES], f32)
        dinv = sb("dinv", [P, TILES], f32)
        dtmp = sb("dtmp", [P, TILES], f32)
        dneg = sb("dneg", [P, TILES], f32)
        conv = sb("conv", [P, B * F], f32)
        stats = sb("stats", [P, B, 6], f32)
        mv = sb("mv", [P, B, 2], f32)
        var = sb("var", [P, B], f32)
        std = sb("std", [P, B], f32)
        rstd = sb("rstd", [P, B], f32)
        ntmp = sb("ntmp", [P, B], f32)
        epsc = sb("epsc", [P, 1], f32)
        warm = sb("warm", [P, 1], f32)

        bank = [ctx.enter_context(nc.psum_tensor(f"bank{n}", [P, HALF], f32)) for n in range(8)]
        turned = bank[0:4]
        second = bank[4:4 + SECOND]
        misc = bank[7]
        lastsum = misc[:, 2 * P:2 * P + TILES - 1]
        product = bank[0:4]
        drow = bank[4:8]

        def turned_of(n):
            return turned[n % 4]

        def second_of(n):
            return second[SECONDS.index(n) % SECOND]

        def x_stage(t):
            return S[:, 7 + t // 2, (t % 2) * B * F:(t % 2 + 1) * B * F].rearrange("p (b f) -> p b f", b=B)

        def xT_stage(k):
            return S[:, TILES - 1, (k % 4) * HALF:(k % 4 + 1) * HALF]

        def diag_of(q):
            return diag[:, :] if q % 3 == 0 else conv[:, (q - 1) * HALF:q * HALF]

        def columns(t):
            return S[:, :, bass.ds(t * P, P)]

        w_loaded = sem("w_loaded")
        x_loaded = [sem(f"x_loaded{t}") for t in range(TILES)]
        adj_loaded = [sem(f"adj_loaded{i}") for i in range(TILES)]
        consts = sem("consts")
        x_turned = sem("x_turned")
        xT_copied = sem("xT_copied")
        hw_done = sem("hw_done")
        hw_kept = sem("hw_kept")
        peak_kept = sem("peak_kept")
        peak_step = sem("peak_step")
        peak_turned = sem("peak_turned")
        peak_spread = sem("peak_spread")
        scale_ready = sem("scale_ready")
        hw_high = sem("hw_high")
        hw_low = sem("hw_low")
        adj_turned = sem("adj_turned")
        sums_done = sem("sums_done")
        relu_done = sem("relu_done")
        s_turned = sem("s_turned")
        last_summed = sem("last_summed")
        mirrored_dve = sem("mirrored_dve")
        mirrored_act = sem("mirrored_act")
        above_summed = sem("above_summed")
        deg_step = sem("deg_step")
        deg_ready = sem("deg_ready")
        root_done = sem("root_done")
        diag_ready = sem("diag_ready")
        drow_ready = sem("drow_ready")
        l_step = sem("l_step")
        l_ready = sem("l_ready")
        l_high = sem("l_high")
        l_low = sem("l_low")
        half_done = sem("half_done")
        quarter_used = sem("quarter_used")
        conv_used = sem("conv_used")
        relu_out = sem("relu_out")
        res_loaded = [sem("res_loaded_even"), sem("res_loaded_odd")]
        n_step = sem("n_step")
        var_ready = sem("var_ready")
        std_ready = sem("std_ready")
        out_ready = sem("out_ready")
        stored = sem("stored")

        def early(k):
            return MIRRORED.index(k) % 3 != 2

        def wait_mirrored(engine, k):
            before = sum(early(m) == early(k) for m in MIRRORED if m < k)
            engine.wait_ge(mirrored_dve if early(k) else mirrored_act, before + 1)

        def wait_turned_read(engine, n):
            kind, k = STEPS[n]
            if kind == "x":
                engine.wait_ge(xT_copied, k + 1)
            else:
                engine.wait_ge(sums_done, k + 1)

        def wait_second_read(engine, n):
            kind, k = STEPS[n]
            if kind == "x":
                engine.wait_ge(hw_kept, k + 1)
            else:
                wait_mirrored(engine, k)

        block = ctx.enter_context(nc.Block())

        @block.sync
        def _(sp):
            for kind, i in arrivals():
                if kind == "x":
                    sp.dma_start(x_stage(i), x_tiles[i]).then_inc(x_loaded[i], 16)
                    if i == 0:
                        sp.dma_start(w_sb[:, :], w).then_inc(w_loaded, 16)
                    continue
                if i == TILES - 1:
                    sp.wait_ge(hw_done, HALVES)
                elif i >= 7:
                    sp.wait_ge(x_turned, 4 * (i - 6))
                sp.dma_start(S[:, i, :], adj_tiles[i]).then_inc(adj_loaded[i], 16)

            def residual(t, parity):
                sp.wait_ge(l_high, 4 * t + 4)
                sp.wait_ge(l_low, 4 * t + 4)
                sp.dma_start(columns(t)[:, 0:B, :], x_tiles[bass.ds(t, 1)].rearrange("t p b f -> (t p) b f"))\
                  .then_inc(res_loaded[parity], 16)

            def store(t):
                sp.wait_ge(out_ready, 2 * t + 2)
                sp.dma_start(out_tiles[bass.ds(t, 1)].rearrange("t p b f -> (t p) b f"), columns(t)[:, B:2 * B, :])\
                  .then_inc(stored, 16)

            residual(0, 0)
            residual(1, 1)
            store(0)
            with sp.Fori(1, TILES - 2, 2) as t:
                residual(t + 1, 0)
                store(t)
                residual(t + 2, 1)
                store(t + 1)
            for half in range(2):
                sp.wait_ge(out_ready, 2 * (TILES - 1) + 1 + half)
                b0 = half * HALF_B
                sp.dma_start(out_tiles[TILES - 1, :, b0:b0 + HALF_B, :],
                             columns(TILES - 1)[:, B + b0:B + b0 + HALF_B, :]).then_inc(stored, 16)
            sp.wait_ge(stored, 16 * (TILES + 1))

        @block.gpsimd
        def _(pool):
            nc.gpsimd.memset(ident[:, :], 0.0).then_inc(consts, 1)
            nc.gpsimd.memset(ones[:, :], 1.0).then_inc(consts, 1)
            nc.gpsimd.memset(rowpart[:, :, :], 0.0).then_inc(consts, 1)
            nc.gpsimd.memset(epsc[:, :], EPS).then_inc(consts, 1)
            pool.wait_ge(consts, 4)
            nc.gpsimd.affine_select(out=ident[:, :], in_=ident[:, :], compare_op=ALU.not_equal, fill=1.0,
                                    base=0, pattern=[[-1, P]], channel_multiplier=1).then_inc(consts, 1)
            nc.gpsimd.memset(above, 0.0).then_inc(above_summed, 1)
            for m, k in enumerate(MIRRORED[:-4]):
                i, j0, nb = GROUPS[k]
                area = above[:, j0:j0 + min(nb, i - j0), :]
                wait_mirrored(pool, k)
                pool.wait_ge(above_summed, m + 1)
                nc.gpsimd.tensor_tensor(area, area, S[:, j0:j0 + min(nb, i - j0), i * P:(i + 1) * P], ALU.add)\
                  .then_inc(above_summed, 1)

        @block.tensor
        def _(pe):
            pe.wait_ge(consts, 5)
            pe.wait_ge(w_loaded, 16)

            def turn_x(n, k):
                t, half = divmod(k, 2)
                pe.wait_ge(x_loaded[t], 16)
                for b in range(HALF_B):
                    last = nc.tensor.transpose(turned_of(n)[:, b * P:(b + 1) * P],
                                               x_stage(t)[:, half * HALF_B + b, :], ident[:, :])
                last.then_inc(x_turned, 1)

            def times_w(n, k):
                pe.wait_ge(xT_copied, k + 1)
                for b in range(HALF_B):
                    last = nc.tensor.matmul(second_of(n)[:, b * F:(b + 1) * F], xT_stage(k)[:, b * P:(b + 1) * P],
                                            w_sb[:, :], start=True, stop=True)
                last.then_inc(hw_done, 1)

            def turn_adj(n, k):
                i, j0, nb = GROUPS[k]
                pe.wait_ge(adj_loaded[j0 + nb - 1], 16)
                for c in range(nb):
                    last = nc.tensor.transpose(turned_of(n)[:, c * P:(c + 1) * P],
                                               S[:, j0 + c, i * P:(i + 1) * P], ident[:, :])
                last.then_inc(adj_turned, 1)

            def turn_s(n, k):
                i, j0, nb = GROUPS[k]
                pe.wait_ge(relu_done, k + 1)
                for c in range(min(nb, i - j0)):
                    block_ij = S[:, i, (j0 + c) * P:(j0 + c + 1) * P]
                    last = nc.tensor.transpose(second_of(n)[:, c * P:(c + 1) * P], block_ij, ident[:, :])
                last.then_inc(s_turned, 1)
                if i == TILES - 1:
                    for c in range(min(nb, i - j0)):
                        block_ij = S[:, i, (j0 + c) * P:(j0 + c + 1) * P]
                        last = nc.tensor.matmul(lastsum[:, j0 + c:j0 + c + 1], block_ij, ones[:, 0:1],
                                                start=True, stop=True)
                    last.then_inc(last_summed, 1)

            for n in range(len(STEPS) + LAG):
                if n == X_END:
                    pe.wait_ge(peak_step, 1)
                    nc.tensor.transpose(misc[0:1, 0:P], peak1[:, :], ident[:, :]).then_inc(peak_turned, 1)
                if n == X_END + 1:
                    pe.wait_ge(peak_step, 2)
                    nc.tensor.matmul(misc[:, P:P + 1], ones[0:1, :], peakall[:, :], start=True, stop=True)\
                      .then_inc(peak_spread, 1)
                if n == len(STEPS) - 1:
                    pe.wait_ge(peak_step, 3)
                if n < len(STEPS):
                    if n >= 4:
                        wait_turned_read(pe, n - 4)
                    kind, k = STEPS[n]
                    (turn_x if kind == "x" else turn_adj)(n, k)
                if n - LAG in SECONDS:
                    kind, k = STEPS[n - LAG]
                    use = SECONDS.index(n - LAG)
                    if use >= SECOND:
                        wait_second_read(pe, SECONDS[use - SECOND])
                    (times_w if kind == "x" else turn_s)(n - LAG, k)

            def spread_d(q):
                pe.wait_ge(diag_ready, q + 1)
                nc.tensor.matmul(drow[q][:, :], ones[:, :], diag_of(q), start=True, stop=True)\
                  .then_inc(drow_ready, 1)

            spread_d(0)

            def quarter(t, parity, q, first=False, halves=(0, 1)):
                pe.wait_ge(l_low, 4 * t + q + 1)
                for m in range(q * QUARTER, (q + 1) * QUARTER):
                    if first:
                        pe.wait_ge(hw_low, 2 * m + 2)
                    for left, part in ((Lh, 0), (Lh, 1), (Ll, 0)):
                        for half in halves:
                            right = Hs[:, 2 * m + half, part * HALF:(part + 1) * HALF]
                            last = nc.tensor.matmul(product[2 * parity + half][:, :], left[:, m, :], right,
                                                    start=(m == 0 and left is Lh and part == 0),
                                                    stop=(m == TILES - 1 and left is Ll))
                return last

            def tile(t, parity, first=False, reuse=True):
                if reuse:
                    pe.wait_ge(relu_out, 2 * t - 2)
                for q in range(4):
                    quarter(t, parity, q, first).then_inc(quarter_used, 1)

            tile(0, 0, first=True, reuse=False)
            for q in range(1, 4):
                spread_d(q)
            tile(1, 1, reuse=False)
            with pe.Fori(2, TILES - 3, 2) as t:
                tile(t, 0)
                tile(t + 1, 1)
            tile(TILES - 2, 0)
            pe.wait_ge(relu_out, 2 * (TILES - 1) - 2)
            for half in range(2):
                for q in range(4):
                    last = quarter(TILES - 1, 1, q, halves=(half,))
                last.then_inc(half_done, 1)

        @block.scalar
        def _(act):
            act.wait_ge(consts, 5)
            nc.scalar.activation(warm[:, :], epsc[:, :], ACT.Sqrt)

            def keep_hw(n, k):
                act.wait_ge(hw_done, k + 1)
                nc.scalar.activation(H[:, k + 2, :], second_of(n)[:, :], ACT.Copy).then_inc(hw_kept, 1)

            def keep_xT(n, k):
                act.wait_ge(x_turned, k + 1)
                if k >= 4:
                    act.wait_ge(hw_done, k - 3)
                nc.scalar.activation(xT_stage(k), turned_of(n)[:, :], ACT.Copy).then_inc(xT_copied, 1)

            def high(k):
                if k >= 2:
                    act.wait_ge(hw_low, k - 1)
                nc.scalar.activation(Hs[:, k, 0:HALF], H[:, k + 2, :], ACT.Copy, scale=hw_scale[:, :])\
                  .then_inc(hw_high, 1)

            def relu(n, k):
                i, j0, nb = GROUPS[k]
                area = S[:, i, j0 * P:(j0 + nb) * P]
                act.wait_ge(sums_done, k + 1)
                nc.scalar.activation(area, area, ACT.Relu, scale=0.5, accum_out=rowpart[:, i, j0 // 4:j0 // 4 + 1])\
                  .then_inc(relu_done, 1)

            def mirror(n, k):
                i, j0, nb = GROUPS[k]
                m, nb = MIRRORED.index(k), min(nb, i - j0)
                act.wait_ge(s_turned, m + 1)
                nc.scalar.activation(S[:, j0:j0 + nb, i * P:(i + 1) * P],
                                     second_of(n)[:, 0:nb * P].rearrange("p (t n) -> p t n", n=P), ACT.Copy)\
                  .then_inc(mirrored_act, 1)

            split = 0
            for n in range(len(STEPS) + LAG + 1):
                if n - LAG - 1 in SECONDS:
                    kind, k = STEPS[n - LAG - 1]
                    if kind == "x":
                        keep_hw(n - LAG - 1, k)
                    elif not early(k):
                        mirror(n - LAG - 1, k)
                if n < len(STEPS):
                    kind, k = STEPS[n]
                    (keep_xT if kind == "x" else relu)(n, k)
                if n > X_END + 2 and (n - X_END) % 2 and split < SPLIT_EARLY:
                    if split == 0:
                        act.wait_ge(scale_ready, 1)
                    high(split)
                    split += 1

            act.wait_ge(deg_ready, 1)
            nc.scalar.activation(droot[:, :], degs[:, :], ACT.Sqrt).then_inc(root_done, 1)

            def l_highs(t, first=False):
                if not first:
                    act.wait_ge(l_ready, t + 4)
                for q in range(4):
                    if first:
                        act.wait_ge(l_ready, q + 1)
                    else:
                        act.wait_ge(quarter_used, 4 * t + q - 3)
                    nc.scalar.activation(Lh[:, q * QUARTER:(q + 1) * QUARTER, :],
                                         columns(t)[:, q * QUARTER:(q + 1) * QUARTER, :], ACT.Copy)\
                      .then_inc(l_high, 1)

            def relu_half(t, parity, half, last=False):
                act.wait_ge(peak_step, 6)
                if last:
                    act.wait_ge(half_done, half + 1)
                else:
                    act.wait_ge(quarter_used, 4 * t + 4)
                nc.scalar.activation(conv[:, half * HALF:(half + 1) * HALF], product[2 * parity + half][:, :],
                                     ACT.Relu, scale=unscale[:, :]).then_inc(relu_out, 1)

            def root_half(t, half):
                part = slice(half * HALF_B, (half + 1) * HALF_B)
                act.wait_ge(var_ready, 2 * t + half + 1)
                nc.scalar.activation(std[:, part], var[:, part], ACT.Sqrt).then_inc(std_ready, 1)

            def norm(t, parity):
                for half in range(2):
                    relu_half(t, parity, half)
                for half in range(2):
                    root_half(t, half)

            l_highs(0, first=True)
            for k in range(split, HALVES):
                high(k)
            l_highs(1)
            act.wait_ge(drow_ready, 4)
            norm(0, 0)
            with act.Fori(1, TILES - 2, 2) as t:
                l_highs(t + 1)
                act.wait_ge(conv_used, 2 * t)
                norm(t, 1)
                l_highs(t + 2)
                act.wait_ge(conv_used, 2 * t + 2)
                norm(t + 1, 0)
            act.wait_ge(conv_used, 2 * (TILES - 1))
            for half in range(2):
                relu_half(TILES - 1, 1, half, last=True)
                root_half(TILES - 1, half)

        @block.vector
        def _(dve):
            def take_peak(k):
                dve.wait_ge(hw_kept, k + 1)
                nc.vector.tensor_reduce(peak[:, k:k + 1], H[:, k + 2, :], AX.X, ALU.max,
                                        apply_absolute_value=True).then_inc(peak_kept, 1)

            def peak_over_tiles():
                dve.wait_ge(peak_kept, HALVES)
                nc.vector.tensor_reduce(peak1[:, :], peak[:, :], AX.X, ALU.max).then_inc(peak_step, 1)

            def peak_over_partitions():
                dve.wait_ge(peak_turned, 1)
                nc.vector.tensor_reduce(peakall[:, :], misc[0:1, 0:P], AX.X, ALU.max).then_inc(peak_step, 1)

            def scales():
                dve.wait_ge(peak_spread, 1)
                nc.vector.tensor_scalar(power[:, :], misc[:, P:P + 1], 2.0 ** -100, 2.0 ** 126, ALU.max, ALU.min)\
                  .then_inc(peak_step, 1)
                dve.wait_ge(peak_step, 3)
                nc.vector.tensor_scalar(power[:, :].bitcast(i32), power[:, :].bitcast(i32), 0x7F800000, None,
                                        ALU.bitwise_and).then_inc(peak_step, 1)
                dve.wait_ge(peak_step, 4)
                nc.vector.tensor_scalar(inverse[:, :].bitcast(i32), power[:, :].bitcast(i32), -1.0,
                                        float(254 << 23), ALU.mult, ALU.add).then_inc(peak_step, 1)
                nc.vector.tensor_scalar(unscale[:, :], power[:, :], 1.0 / (HW_TOP * L_SCALE), None, ALU.mult)\
                  .then_inc(peak_step, 1)
                dve.wait_ge(peak_step, 6)
                nc.vector.tensor_scalar(hw_scale[:, :], inverse[:, :], HW_TOP, None, ALU.mult).then_inc(scale_ready, 1)

            def low(k):
                dve.wait_ge(hw_high, k + 1)
                nc.vector.scalar_tensor_tensor(out=Hs[:, k, HALF:2 * HALF], in0=H[:, k + 2, :],
                                               scalar=hw_scale[:, :], in1=Hs[:, k, 0:HALF],
                                               op0=ALU.mult, op1=ALU.subtract).then_inc(hw_low, 1)

            def add(n, k):
                i, j0, nb = GROUPS[k]
                area = S[:, i, j0 * P:(j0 + nb) * P]
                dve.wait_ge(adj_loaded[i], 16)
                dve.wait_ge(adj_turned, k + 1)
                nc.vector.tensor_tensor(area, area, turned_of(n)[:, 0:nb * P], ALU.add).then_inc(sums_done, 1)

            def mirror(n, k):
                i, j0, nb = GROUPS[k]
                m, nb = MIRRORED.index(k), min(nb, i - j0)
                dve.wait_ge(s_turned, m + 1)
                nc.vector.tensor_copy(S[:, j0:j0 + nb, i * P:(i + 1) * P],
                                      second_of(n)[:, 0:nb * P].rearrange("p (t n) -> p t n", n=P))\
                  .then_inc(mirrored_dve, 1)

            split = 0
            for n in range(len(STEPS) + LAG + 1):
                if n == X_END:
                    peak_over_tiles()
                if n == X_END + 1:
                    peak_over_partitions()
                if n == X_END + 2:
                    scales()
                if n - LAG - 1 in SECONDS:
                    kind, k = STEPS[n - LAG - 1]
                    if kind == "adj" and early(k):
                        mirror(n - LAG - 1, k)
                if n < len(STEPS) and STEPS[n][0] == "adj":
                    add(n, STEPS[n][1])
                if n >= LAG + 2 and n - LAG - 2 < len(STEPS) and STEPS[n - LAG - 2][0] == "x":
                    take_peak(STEPS[n - LAG - 2][1])
                if n > X_END + 3 and (n - X_END) % 2 == 0 and split < SPLIT_EARLY:
                    if split == 0:
                        dve.wait_ge(scale_ready, 1)
                    low(split)
                    split += 1
                if n == len(STEPS) - 1:
                    dve.wait_ge(above_summed, 1 + len(MIRRORED) - 4)
                    nc.vector.tensor_reduce(dhigh[:, :], above, AX.X, ALU.add).then_inc(deg_step, 1)

            dve.wait_ge(relu_done, len(GROUPS))
            nc.vector.tensor_reduce(dlow[:, :], rowpart[:, :, :], AX.X, ALU.add).then_inc(deg_step, 1)
            dve.wait_ge(deg_step, 2)
            nc.vector.tensor_tensor(deg[:, :], dlow[:, :], dhigh[:, :], ALU.add).then_inc(deg_step, 1)
            dve.wait_ge(deg_step, 3)
            dve.wait_ge(last_summed, 4)
            nc.vector.tensor_tensor(deg[:, 0:TILES - 1], deg[:, 0:TILES - 1], lastsum, ALU.add).then_inc(deg_step, 1)
            dve.wait_ge(deg_step, 4)
            nc.vector.scalar_tensor_tensor(out=degs[:, :], in0=deg[:, :], scalar=0.0, in1=deg[:, :],
                                           op0=ALU.is_le, op1=ALU.add).then_inc(deg_ready, 1)
            dve.wait_ge(root_done, 1)
            nc.vector.reciprocal(dinv[:, :], droot[:, :]).then_inc(deg_step, 1)
            dve.wait_ge(deg_step, 5)
            nc.vector.tensor_tensor(dtmp[:, :], dinv[:, :], dinv[:, :], ALU.mult).then_inc(deg_step, 1)
            dve.wait_ge(deg_step, 6)
            nc.vector.tensor_tensor(dtmp[:, :], dtmp[:, :], degs[:, :], ALU.mult).then_inc(deg_step, 1)
            dve.wait_ge(deg_step, 7)
            nc.vector.tensor_scalar(dtmp[:, :], dtmp[:, :], -0.5, 1.5, ALU.mult, ALU.add).then_inc(deg_step, 1)
            dve.wait_ge(deg_step, 8)
            nc.vector.tensor_tensor(dinv[:, :], dinv[:, :], dtmp[:, :], ALU.mult).then_inc(deg_step, 1)
            dve.wait_ge(deg_step, 9)
            nc.vector.scalar_tensor_tensor(out=dinv[:, :], in0=deg[:, :], scalar=0.0, in1=dinv[:, :],
                                           op0=ALU.is_gt, op1=ALU.mult).then_inc(deg_step, 1)
            dve.wait_ge(deg_step, 10)
            nc.vector.tensor_scalar(dneg[:, :], dinv[:, :], -L_SCALE, None, ALU.mult).then_inc(deg_step, 1)
            dve.wait_ge(deg_step, 11)

            def diagonal(q):
                nc.vector.tensor_tensor(diag_of(q).rearrange("p (t n) -> p t n", n=P),
                                        ident[:, :].unsqueeze(1).to_broadcast([P, 4, P]),
                                        dneg[:, 4 * q:4 * q + 4].unsqueeze(2).to_broadcast([P, 4, P]), ALU.mult)\
                  .then_inc(diag_ready, 1)

            diagonal(0)

            def l_left(t, rows):
                part = columns(t)[:, rows, :]
                nc.vector.tensor_tensor(part, part,
                                        dinv[:, rows].unsqueeze(2).to_broadcast([P, part.shape[1], P]), ALU.mult)\
                  .then_inc(l_step, 1)

            def l_right(t, rows):
                part = columns(t)[:, rows, :]
                d_n = drow[t // 4][:, t % 4 * P:(t % 4 + 1) * P]
                return nc.vector.tensor_tensor(part, part, d_n.unsqueeze(1).to_broadcast([P, part.shape[1], P]),
                                               ALU.mult)

            def l_diagonal(t):
                block_tt = S[:, t, t * P:(t + 1) * P]
                return nc.vector.scalar_tensor_tensor(out=block_tt, in0=ident[:, :], scalar=L_SCALE, in1=block_tt,
                                                      op0=ALU.mult, op1=ALU.add)

            def l_tile(t):
                rows = slice(0, TILES)
                l_left(t, rows)
                dve.wait_ge(l_step, 2 * t + 4)
                l_right(t, rows).then_inc(l_step, 1)
                dve.wait_ge(l_step, 2 * t + 5)
                l_diagonal(t).then_inc(l_ready, 1)

            def l_low_quarter(t, q):
                dve.wait_ge(l_high, 4 * t + q + 1)
                part = slice(q * QUARTER, (q + 1) * QUARTER)
                nc.vector.tensor_tensor(Ll[:, part, :], columns(t)[:, part, :], Lh[:, part, :], ALU.subtract)\
                  .then_inc(l_low, 1)

            def l_lows(t):
                for q in range(4):
                    l_low_quarter(t, q)

            N_STEPS = 7

            def norm_half(t, half):
                part = slice(half * HALF_B, (half + 1) * HALF_B)
                rows = columns(t)[:, B + half * HALF_B:B + (half + 1) * HALF_B, :]
                n0 = (2 * t + half) * N_STEPS
                dve.wait_ge(relu_out, 2 * t + half + 1)
                dve.wait_ge(res_loaded[t % 2], 16 * (t // 2 + 1))
                nc.vector.tensor_tensor(rows, conv[:, half * HALF:(half + 1) * HALF].rearrange("p (b f) -> p b f", f=F),
                                        columns(t)[:, part, :], ALU.add).then_inc(conv_used, 1)
                dve.wait_ge(conv_used, 2 * t + half + 1)
                for b in range(HALF_B):
                    last = nc.vector.bn_stats(stats[:, half * HALF_B + b, :], rows[:, b, :])
                last.then_inc(n_step, 1)
                dve.wait_ge(n_step, n0 + 1)
                for b in range(HALF_B):
                    last = nc.vector.bn_aggr(mv[:, half * HALF_B + b, :], stats[:, half * HALF_B + b, :])
                last.then_inc(n_step, 1)
                dve.wait_ge(n_step, n0 + 2)
                nc.vector.tensor_scalar(var[:, part], mv[:, part, 1], EPS, None, ALU.add).then_inc(var_ready, 1)
                dve.wait_ge(std_ready, 2 * t + half + 1)
                nc.vector.reciprocal(rstd[:, part], std[:, part]).then_inc(n_step, 1)
                dve.wait_ge(n_step, n0 + 3)
                nc.vector.tensor_tensor(ntmp[:, part], rstd[:, part], rstd[:, part], ALU.mult).then_inc(n_step, 1)
                dve.wait_ge(n_step, n0 + 4)
                nc.vector.tensor_tensor(ntmp[:, part], ntmp[:, part], var[:, part], ALU.mult).then_inc(n_step, 1)
                dve.wait_ge(n_step, n0 + 5)
                nc.vector.tensor_scalar(ntmp[:, part], ntmp[:, part], -0.5, 1.5, ALU.mult, ALU.add)\
                  .then_inc(n_step, 1)
                dve.wait_ge(n_step, n0 + 6)
                nc.vector.tensor_tensor(rstd[:, part], rstd[:, part], ntmp[:, part], ALU.mult).then_inc(n_step, 1)
                dve.wait_ge(n_step, n0 + 7)
                for b in range(HALF_B):
                    at = half * HALF_B + b
                    last = nc.vector.tensor_scalar(rows[:, b, :], rows[:, b, :], mv[:, at, 0:1], rstd[:, at:at + 1],
                                                   ALU.subtract, ALU.mult)
                last.then_inc(out_ready, 1)

            quarters = [slice(q * QUARTER, (q + 1) * QUARTER) for q in range(4)]
            for rows in quarters:
                l_left(0, rows)
            dve.wait_ge(drow_ready, 1)
            dve.wait_ge(l_step, 1)
            l_right(0, quarters[0]).then_inc(l_step, 1)
            dve.wait_ge(l_step, 5)
            l_diagonal(0).then_inc(l_ready, 1)
            for q in range(1, 4):
                l_right(0, quarters[q]).then_inc(l_ready, 1)
                l_low_quarter(0, q - 1)
            l_low_quarter(0, 3)
            for q in range(1, 4):
                diagonal(q)
            for k in range(split, HALVES):
                low(k)
            for t in range(1, TILES):
                if t == 4:
                    dve.wait_ge(drow_ready, 4)
                l_tile(t)
                l_lows(t)
                for half in range(2):
                    norm_half(t - 1, half)
            for half in range(2):
                norm_half(TILES - 1, half)


def kernel(x, adj, L0_gnn_W):
    import numpy as np
    import concourse.bacc as bacc
    from concourse.bass_utils import run_bass_kernel_spmd

    nc = bacc.Bacc("TRN2", target_bir_lowering=False, num_devices=1, dynamic_dma_scratch_size=1024)
    arrays, args = {}, []
    for name, a in (("x", x), ("adj", adj), ("L0_gnn_W", L0_gnn_W)):
        a = np.ascontiguousarray(a)
        arrays[f"in_{name}"] = a
        args.append(nc.dram_tensor(f"in_{name}", a.shape, mybir.dt.from_np(a.dtype), kind="ExternalInput").ap())
    args.append(nc.dram_tensor("out", (B, N, F), mybir.dt.float32, kind="ExternalOutput").ap())
    gcn_layernorm(nc, *args)
    return run_bass_kernel_spmd(nc, [arrays], core_ids=[0]).results[0]["out"]
```

```python
from contextlib import ExitStack

import concourse.bass as bass
from concourse import mybir

B, N, F = 8, 2048, 128
P = 128
TILES = N // P
HALF_B = B // 2
HALF = HALF_B * F
HALVES = 2 * TILES
EPS = 1e-5
L_SCALE = 2.0 ** 15
HW_TOP = 2.0 ** 13
LEAD = 4
X_EVERY = 2
LAG = 3
BEHIND = 2
QUARTER = TILES // 4
SECOND = 3
SUMS_BY_PE = 14
MIRRORS_SHARED = 32
AHEAD = 4
SPLIT_BEFORE_L = 5
SPLIT_IN_L = 12
POOL_FIRST = 4
POOL_EVERY, POOL_SET = 5, (0, 3)
L1_FROM = 13
LAST_PIECES = [(0, 4), (4, 2), (6, 2)]


def runs(i, first, last):
    return [(i, j0, min(4, last + 1 - j0)) for j0 in range(first, last + 1, 4)]


def adj_units():
    h = TILES // 2
    units = [((i, 0), runs(i, 0, i)) for i in range(h)]
    for s in range(h):
        units.append(((s, 1), runs(s, h, h + s - 1)))
        units.append(((h + s, 0), runs(h + s, 0, s)))
    return units + [((i, 1), runs(i, h, i)) for i in range(h, TILES)]


def arrivals():
    order = [("x", t, []) for t in range(LEAD)]
    t = LEAD
    for n, (unit, groups) in enumerate(adj_units()):
        order.append(("adj", unit, groups))
        while t < TILES and (t - LEAD + 1) * X_EVERY <= n + 1:
            order.append(("x", t, []))
            t += 1
    return order


def steps():
    order, k = [], 0
    for kind, what, groups in arrivals():
        if kind == "x":
            order += [("x", 2 * what), ("x", 2 * what + 1)]
        for _ in groups:
            order.append(("adj", k))
            k += 1
    return order


def gcn_layernorm(nc, x, adj, w, out):
    f32, f16, i32 = mybir.dt.float32, mybir.dt.float16, mybir.dt.int32
    ALU, ACT, AX = mybir.AluOpType, mybir.ActivationFunctionType, mybir.AxisListType

    x_tiles = x.rearrange("b (t p) f -> t p b f", p=P)
    out_tiles = out.rearrange("b (t p) f -> t p b f", p=P)
    adj_tiles = adj.rearrange("(t p) n -> t p n", p=P)

    GROUPS = [group for _, _, groups in arrivals() for group in groups]

    X_PLACES = TILES // 2 - 2

    def off_diagonal(k):
        i, j0, nb = GROUPS[k]
        return nb - 1 if j0 <= i < j0 + nb else nb

    MIRRORED = [k for k in range(len(GROUPS)) if off_diagonal(k)]
    PE_SUMS = [k for k in MIRRORED if GROUPS[k][0] >= SUMS_BY_PE and GROUPS[k][1] >= TILES // 2]
    POOL_SUMS = [k for k in MIRRORED if k not in PE_SUMS]
    STEPS = steps()
    UPPER = TILES // 2
    FIRST_OF_LAST = GROUPS.index((UPPER, UPPER, 1))
    LAST_QUARTER_STEP = STEPS.index(("adj", FIRST_OF_LAST))
    SUMS_STEP = STEPS.index(("adj", PE_SUMS[0]))
    X_END = max(n for n, (kind, _) in enumerate(STEPS) if kind == "x") + LAG + 3
    SCALES_STEP = X_END + 2 * BEHIND + 2
    EARLY = range(SCALES_STEP + 1, len(STEPS) + LAG, 2)
    SECONDS = [n for n, (kind, k) in enumerate(STEPS) if kind == "x" or k in MIRRORED]

    ctx = ExitStack()
    with ctx:
        def sb(name, shape, dt):
            return ctx.enter_context(nc.sbuf_tensor(name, shape, dt))

        def sem(name):
            return ctx.enter_context(nc.semaphore(name))

        S = sb("S", [P, TILES, N], f32)
        H = sb("H", [P, HALVES + AHEAD, HALF], f32)
        Hs = H[:, :, :].bitcast(f16)
        L16 = sb("L16", [P, 2, TILES, P], f16)
        Lh, Ll = L16[:, 0], L16[:, 1]
        above = L16[:, :, :, :].rearrange("p a t n -> p (a t n)").bitcast(f32)\
                               .rearrange("p (t n) -> p t n", n=P)
        ident = sb("ident", [P, P], f32)
        ones = sb("ones", [P, P], f32)
        w_sb = sb("w_sb", [P, F], f32)
        minus = sb("minus", [P, P], f32)
        peak = sb("peak", [P, HALVES], f32)
        peak1 = sb("peak1", [P, 1], f32)
        peakrow = sb("peakrow", [1, P], f32)
        peakall = sb("peakall", [1, 1], f32)
        power = sb("power", [P, 1], f32)
        inverse = sb("inverse", [P, 1], f32)
        hw_scale = sb("hw_scale", [P, 1], f32)
        unscale = sb("unscale", [P, 1], f32)
        rowpart = sb("rowpart", [P, TILES, 4], f32)
        dlow = sb("dlow", [P, TILES], f32)
        dhigh = sb("dhigh", [P, TILES], f32)
        dlast = sb("dlast", [P, TILES], f32)
        deg = sb("deg", [P, TILES], f32)
        degs = sb("degs", [P, TILES], f32)
        droot = sb("droot", [P, TILES], f32)
        dinv = sb("dinv", [P, TILES], f32)
        dtmp = sb("dtmp", [P, TILES], f32)
        dmask = sb("dmask", [P, TILES], f32)
        conv = sb("conv", [P, B * F], f32)
        stats = sb("stats", [P, B, 6], f32)
        mean = sb("mean", [P, B], f32)
        apart = sb("apart", [P, B], f32)
        squares = sb("squares", [P, B], f32)
        var = sb("var", [P, B], f32)
        std = sb("std", [P, B], f32)
        rstd = sb("rstd", [P, B], f32)
        ntmp = sb("ntmp", [P, B], f32)
        epsc = sb("epsc", [P, 1], f32)
        warm = sb("warm", [P, 1], f32)

        low_banks = [ctx.enter_context(nc.psum_tensor(f"bank{n}", [P, HALF], f32)) for n in range(4)]
        high_banks = ctx.enter_context(nc.psum_tensor("high_banks", [P, 4, HALF], f32))
        bank = [b[:, :] for b in low_banks] + [high_banks[:, n, :] for n in range(4)]
        turned = bank[0:4]
        second = bank[4:4 + SECOND]
        misc = bank[7]
        lastsum = misc[:, 2 * P:2 * P + (TILES - SUMS_BY_PE) * TILES].rearrange("p (j i) -> p j i", j=TILES)
        product = bank[0:4]

        d_rows = high_banks[:, :, :].rearrange("p a (b n) -> p (a b) n", n=P)

        def drow(t, parity):
            return d_rows[:, bass.ds(parity * (TILES // 2) + (t - parity) // 2, 1), :]

        def turned_of(n):
            return turned[n % 4]

        def second_of(n):
            return second[SECONDS.index(n) % SECOND]

        def x_place(t):
            return (t + 2) % X_PLACES

        def x_stage(t):
            return S[:, TILES // 2 + x_place(t), N // 2:N].rearrange("p (b f) -> p b f", b=B)

        def xT_stage(k):
            return S[:, TILES - 2 + k % 4 // 2, N // 2 + k % 2 * HALF:N // 2 + (k % 2 + 1) * HALF]

        def last_product(piece):
            return [product[2], product[3], product[0]][piece][:, 0:LAST_PIECES[piece][1] * F]

        def columns(t):
            return S[:, :, bass.ds(t * P, P)]

        w_loaded = sem("w_loaded")
        x_first = sem("x_first")
        x_loaded = [sem(f"x_loaded{t}") for t in range(TILES)]
        adj_loaded = [[sem(f"adj_loaded{i}_{h}") for h in range(2)] for i in range(TILES)]
        consts = sem("consts")
        x_turned = sem("x_turned")
        xT_copied = sem("xT_copied")
        hw_done = sem("hw_done")
        hw_kept = sem("hw_kept")
        peak_kept = sem("peak_kept")
        peak_step = sem("peak_step")
        peak_turned = sem("peak_turned")
        peak_spread = sem("peak_spread")
        scale_ready = sem("scale_ready")
        hw_high = sem("hw_high")
        hw_low = sem("hw_low")
        adj_turned = sem("adj_turned")
        sums_done = sem("sums_done")
        relu_done = sem("relu_done")
        s_turned = sem("s_turned")
        sums_cleared = sem("sums_cleared")
        last_summed = sem("last_summed")
        mirrored_dve = sem("mirrored_dve")
        mirrored_act = sem("mirrored_act")
        hw_scaled = sem("hw_scaled")
        hw_low_pool = sem("hw_low_pool")
        above_summed = sem("above_summed")
        deg_step = sem("deg_step")
        deg_ready = sem("deg_ready")
        root_done = sem("root_done")
        d_ready = sem("d_ready")
        drow_ready = sem("drow_ready")
        l_step = sem("l_step")
        l_ready = sem("l_ready")
        l_high = sem("l_high")
        l_low = sem("l_low")
        piece_done = sem("piece_done")
        quarter_used = sem("quarter_used")
        res_added = sem("res_added")
        relu_out = sem("relu_out")
        res_loaded = [sem("res_loaded_even"), sem("res_loaded_odd")]
        n_step = sem("n_step")
        var_ready = sem("var_ready")
        std_ready = sem("std_ready")
        out_ready = sem("out_ready")
        stored = sem("stored")

        def mirror_by_dve(k):
            m = MIRRORED.index(k)
            return m % 2 == 0 and m < MIRRORS_SHARED

        def wait_mirrored(engine, k):
            before = sum(mirror_by_dve(m) == mirror_by_dve(k) for m in MIRRORED if m < k)
            engine.wait_ge(mirrored_dve if mirror_by_dve(k) else mirrored_act, before + 1)

        def by_pool(k):
            return k < POOL_FIRST or k % POOL_EVERY in POOL_SET

        def wait_low(engine, k):
            if by_pool(k):
                engine.wait_ge(hw_low_pool, sum(by_pool(m) for m in range(k + 1)))
            else:
                engine.wait_ge(hw_low, sum(not by_pool(m) for m in range(k + 1)))

        def wait_turned_read(engine, n):
            kind, k = STEPS[n]
            if kind == "x":
                engine.wait_ge(xT_copied, k + 1)
            else:
                engine.wait_ge(sums_done, k + 1)

        def wait_second_read(engine, n):
            kind, k = STEPS[n]
            if kind == "x":
                engine.wait_ge(hw_kept, k + 1)
            else:
                wait_mirrored(engine, k)

        block = ctx.enter_context(nc.Block())

        @block.sync
        def _(sp):
            for kind, what, _ in arrivals():
                if kind == "x":
                    t = what
                    if t == 0:
                        sp.dma_start(x_stage(0)[:, 0:HALF_B, :], x_tiles[0, :, 0:HALF_B, :]).then_inc(x_first, 16)
                        sp.dma_start(x_stage(0)[:, HALF_B:B, :], x_tiles[0, :, HALF_B:B, :]).then_inc(x_loaded[0], 16)
                        continue
                    if t >= X_PLACES:
                        sp.wait_ge(x_turned, 2 * (t - X_PLACES) + 2)
                    sp.dma_start(x_stage(t), x_tiles[t]).then_inc(x_loaded[t], 16)
                else:
                    i, h = what
                    if h == 1 and i >= TILES - 2:
                        sp.wait_ge(hw_done, HALVES)
                    elif h == 1 and i >= TILES // 2:
                        sp.wait_ge(x_turned, 2 * (TILES - X_PLACES + i - TILES // 2) + 2)
                    cols = slice(h * (N // 2), (h + 1) * (N // 2))
                    sp.dma_start(S[:, i, cols], adj_tiles[i, :, cols])\
                      .then_inc(adj_loaded[i][h], 16)

            def residual(t, parity):
                sp.wait_ge(l_high, 4 * t + 4)
                sp.wait_ge(l_low, 4 * t + 4)
                sp.dma_start(columns(t)[:, 0:B, :], x_tiles[bass.ds(t, 1)].rearrange("t p b f -> (t p) b f"))\
                  .then_inc(res_loaded[parity], 16)

            def store(t):
                sp.wait_ge(out_ready, 2 * t + 2)
                sp.dma_start(out_tiles[bass.ds(t, 1)].rearrange("t p b f -> (t p) b f"), columns(t)[:, B:2 * B, :])\
                  .then_inc(stored, 16)

            residual(0, 0)
            residual(1, 1)
            store(0)
            with sp.Fori(1, TILES - 2, 2) as t:
                residual(t + 1, 0)
                store(t)
                residual(t + 2, 1)
                store(t + 1)
            for piece, (b0, nb) in enumerate(LAST_PIECES):
                sp.wait_ge(out_ready, 2 * (TILES - 1) + 1 + piece)
                sp.dma_start(out_tiles[TILES - 1, :, b0:b0 + nb, :],
                             columns(TILES - 1)[:, B + b0:B + b0 + nb, :]).then_inc(stored, 16)
            sp.wait_ge(stored, 16 * (TILES - 1 + len(LAST_PIECES)))

        @block.gpsimd
        def _(pool):
            nc.gpsimd.memset(ident[:, :], 0.0).then_inc(consts, 1)
            nc.gpsimd.memset(ones[:, :], 1.0).then_inc(consts, 1)
            nc.gpsimd.memset(rowpart[:, :, :], 0.0).then_inc(consts, 1)
            nc.gpsimd.memset(epsc[:, :], EPS).then_inc(consts, 1)
            nc.gpsimd.memset(minus[:, :], 0.0).then_inc(consts, 1)
            pool.wait_ge(consts, 5)
            nc.gpsimd.affine_select(out=ident[:, :], in_=ident[:, :], compare_op=ALU.not_equal, fill=1.0,
                                    base=0, pattern=[[-1, P]], channel_multiplier=1).then_inc(consts, 1)
            nc.gpsimd.affine_select(out=minus[:, :], in_=minus[:, :], compare_op=ALU.not_equal, fill=-L_SCALE,
                                    base=0, pattern=[[-1, P]], channel_multiplier=1).then_inc(consts, 1)
            nc.gpsimd.memset(above, 0.0).then_inc(above_summed, 1)
            for m, k in enumerate(POOL_SUMS):
                i, j0, nb = GROUPS[k]
                nb = off_diagonal(k)
                area = above[:, j0:j0 + nb, :]
                wait_mirrored(pool, k)
                pool.wait_ge(above_summed, m + 1)
                nc.gpsimd.tensor_tensor(area, area, S[:, j0:j0 + nb, i * P:(i + 1) * P], ALU.add)\
                  .then_inc(above_summed, 1)

            pool.wait_ge(scale_ready, 1)
            mine = [k for k in range(HALVES) if by_pool(k)]
            nc.gpsimd.tensor_scalar(H[:, mine[0] + AHEAD, :], H[:, mine[0] + AHEAD, :], hw_scale[:, :], 1.0,
                                    ALU.mult, ALU.mult).then_inc(hw_scaled, 1)
            for n, k in enumerate(mine):
                if n + 1 < len(mine):
                    after = H[:, mine[n + 1] + AHEAD, :]
                    nc.gpsimd.tensor_scalar(after, after, hw_scale[:, :], 1.0, ALU.mult, ALU.mult)\
                      .then_inc(hw_scaled, 1)
                pool.wait_ge(hw_scaled, n + 1)
                pool.wait_ge(hw_high, k + 1)
                nc.gpsimd.tensor_tensor(Hs[:, k, HALF:2 * HALF], H[:, k + AHEAD, :], Hs[:, k, 0:HALF], ALU.subtract)\
                  .then_inc(hw_low_pool, 1)

        @block.tensor
        def _(pe):
            pe.wait_ge(consts, 7)

            def turn_x(n, k):
                t, half = divmod(k, 2)
                pe.wait_ge(x_first if k == 0 else x_loaded[t], 16)
                for b in range(HALF_B):
                    last = nc.tensor.transpose(turned_of(n)[:, b * P:(b + 1) * P],
                                               x_stage(t)[:, half * HALF_B + b, :], ident[:, :])
                last.then_inc(x_turned, 1)

            def times_w(n, k):
                pe.wait_ge(w_loaded, 16)
                pe.wait_ge(xT_copied, k + 1)
                for b in range(HALF_B):
                    last = nc.tensor.matmul(second_of(n)[:, b * F:(b + 1) * F], xT_stage(k)[:, b * P:(b + 1) * P],
                                            w_sb[:, :], start=True, stop=True)
                last.then_inc(hw_done, 1)

            def turn_adj(n, k):
                i, j0, nb = GROUPS[k]
                pe.wait_ge(adj_loaded[j0 + nb - 1][i // (TILES // 2)], 16)
                for c in range(nb):
                    last = nc.tensor.transpose(turned_of(n)[:, c * P:(c + 1) * P],
                                               S[:, j0 + c, i * P:(i + 1) * P], ident[:, :])
                last.then_inc(adj_turned, 1)

            def turn_s(n, k):
                i, j0, nb = GROUPS[k]
                pe.wait_ge(relu_done, k + 1)
                for c in range(off_diagonal(k)):
                    block_ij = S[:, i, (j0 + c) * P:(j0 + c + 1) * P]
                    last = nc.tensor.transpose(second_of(n)[:, c * P:(c + 1) * P], block_ij, ident[:, :])
                last.then_inc(s_turned, 1)
                if k in PE_SUMS:
                    for c in range(off_diagonal(k)):
                        block_ij = S[:, i, (j0 + c) * P:(j0 + c + 1) * P]
                        to = i - SUMS_BY_PE
                        last = nc.tensor.matmul(lastsum[:, j0 + c, to:to + 1], block_ij, ones[:, 0:1],
                                                start=True, stop=True)
                    last.then_inc(last_summed, 1)

            for n in range(len(STEPS) + LAG):
                if n == X_END + BEHIND:
                    pe.wait_ge(peak_step, 1)
                    nc.tensor.transpose(misc[0:1, 0:P], peak1[:, :], ident[:, :]).then_inc(peak_turned, 1)
                if n == X_END + 2 * BEHIND + 1:
                    pe.wait_ge(peak_step, 2)
                    nc.tensor.matmul(misc[:, P:P + 1], ones[0:1, :], peakall[:, :], start=True, stop=True)\
                      .then_inc(peak_spread, 1)
                if n - LAG == SUMS_STEP:
                    pe.wait_ge(sums_cleared, 1)
                    pe.wait_ge(peak_step, 3)
                if n < len(STEPS):
                    if n >= 4:
                        wait_turned_read(pe, n - 4)
                    kind, k = STEPS[n]
                    (turn_x if kind == "x" else turn_adj)(n, k)
                if n - LAG in SECONDS:
                    kind, k = STEPS[n - LAG]
                    use = SECONDS.index(n - LAG)
                    if use >= SECOND:
                        wait_second_read(pe, SECONDS[use - SECOND])
                    (times_w if kind == "x" else turn_s)(n - LAG, k)

            def spread_d(t):
                nc.tensor.matmul(drow(t, t % 2).rearrange("p o n -> p (o n)"), dinv[:, t:t + 1].to_broadcast([P, P]),
                                 minus[:, :], start=True, stop=True).then_inc(drow_ready, 1)

            pe.wait_ge(d_ready, 1)
            spread_d(0)
            pe.wait_ge(mirrored_act, sum(not mirror_by_dve(k) for k in MIRRORED))
            spread_d(1)

            def quarter(t, parity, q, first=False):
                pe.wait_ge(l_low, 4 * t + q + 1)
                for m in range(q * QUARTER, (q + 1) * QUARTER):
                    if first:
                        wait_low(pe, 2 * m + 1)
                        wait_low(pe, 2 * m)
                    for left, part in ((Lh, 0), (Lh, 1), (Ll, 0)):
                        for half in range(2):
                            right = Hs[:, 2 * m + half, part * HALF:(part + 1) * HALF]
                            last = nc.tensor.matmul(product[2 * parity + half][:, :], left[:, m, :], right,
                                                    start=(m == 0 and left is Lh and part == 0),
                                                    stop=(m == TILES - 1 and left is Ll))
                return last

            def tile(t, parity, first=False, reuse=True):
                if reuse:
                    pe.wait_ge(relu_out, 2 * t - 2)
                for q in range(4):
                    quarter(t, parity, q, first).then_inc(quarter_used, 1)

            tile(0, 0, first=True, reuse=False)
            pe.wait_ge(l_ready, 5)
            for t in range(2, TILES):
                spread_d(t)
            tile(1, 1, reuse=False)
            with pe.Fori(2, TILES - 3, 2) as t:
                tile(t, 0)
                tile(t + 1, 1)
            tile(TILES - 2, 0)
            for piece, (b0, nb) in enumerate(LAST_PIECES):
                pe.wait_ge(relu_out, 2 * (TILES - 2) + (1 if piece == 2 else 0))
                for m in range(TILES):
                    if piece == 0 and m % QUARTER == 0:
                        pe.wait_ge(l_low, 4 * (TILES - 1) + m // QUARTER + 1)
                    for left, part in ((Lh, 0), (Lh, 1), (Ll, 0)):
                        at = part * HALF + b0 % HALF_B * F
                        last = nc.tensor.matmul(last_product(piece), left[:, m, :],
                                                Hs[:, 2 * m + b0 // HALF_B, at:at + nb * F],
                                                start=(m == 0 and left is Lh and part == 0),
                                                stop=(m == TILES - 1 and left is Ll))
                last.then_inc(piece_done, 1)

        @block.scalar
        def _(act):
            act.dma_start(w_sb[:, :], w).then_inc(w_loaded, 16)
            act.wait_ge(consts, 7)
            nc.scalar.activation(warm[:, :], epsc[:, :], ACT.Sqrt)

            def keep_hw(n, k):
                act.wait_ge(hw_done, k + 1)
                nc.scalar.activation(H[:, k + AHEAD, :], second_of(n)[:, :], ACT.Copy).then_inc(hw_kept, 1)

            def keep_xT(n, k):
                act.wait_ge(x_turned, k + 1)
                if k >= 4:
                    act.wait_ge(hw_done, k - 3)
                nc.scalar.activation(xT_stage(k), turned_of(n)[:, :], ACT.Copy).then_inc(xT_copied, 1)

            def high(k):
                if k >= AHEAD:
                    wait_low(act, k - AHEAD)
                if by_pool(k):
                    act.wait_ge(hw_scaled, sum(by_pool(m) for m in range(k + 1)))
                    nc.scalar.activation(Hs[:, k, 0:HALF], H[:, k + AHEAD, :], ACT.Copy).then_inc(hw_high, 1)
                    return
                nc.scalar.activation(Hs[:, k, 0:HALF], H[:, k + AHEAD, :], ACT.Copy, scale=hw_scale[:, :])\
                  .then_inc(hw_high, 1)

            def relu(n, k):
                i, j0, nb = GROUPS[k]
                area = S[:, i, j0 * P:(j0 + nb) * P]
                act.wait_ge(sums_done, k + 1)
                nc.scalar.activation(area, area, ACT.Relu, scale=0.5, accum_out=rowpart[:, i, j0 // 4:j0 // 4 + 1])\
                  .then_inc(relu_done, 1)

            def mirror(n, k):
                i, j0, nb = GROUPS[k]
                m, nb = MIRRORED.index(k), off_diagonal(k)
                act.wait_ge(s_turned, m + 1)
                nc.scalar.activation(S[:, j0:j0 + nb, i * P:(i + 1) * P],
                                     second_of(n)[:, 0:nb * P].rearrange("p (t n) -> p t n", n=P), ACT.Copy)\
                  .then_inc(mirrored_act, 1)

            for n in range(len(STEPS) + LAG + 1):
                if n - LAG - 1 in SECONDS:
                    kind, k = STEPS[n - LAG - 1]
                    if kind == "x":
                        keep_hw(n - LAG - 1, k)
                    elif not mirror_by_dve(k):
                        mirror(n - LAG - 1, k)
                if n < len(STEPS):
                    kind, k = STEPS[n]
                    (keep_xT if kind == "x" else relu)(n, k)
                if n in EARLY:
                    act.wait_ge(scale_ready, 1)
                    high(EARLY.index(n))

            act.wait_ge(deg_ready, 1)
            nc.scalar.activation(droot[:, :], degs[:, :], ACT.Sqrt).then_inc(root_done, 1)

            def highs_to(k):
                for m in range(highs_to.done, k):
                    high(m)
                highs_to.done = max(highs_to.done, k)

            highs_to.done = len(EARLY)

            def l_highs(t, first=False):
                if not first:
                    act.wait_ge(l_ready, t + 4)
                for q in range(4):
                    if first:
                        if q == 0:
                            highs_to(SPLIT_BEFORE_L)
                        if q == 2:
                            highs_to(SPLIT_IN_L)
                        act.wait_ge(l_ready, q + 1)
                    else:
                        act.wait_ge(quarter_used, 4 * t + q - 3)
                    nc.scalar.activation(Lh[:, q * QUARTER:(q + 1) * QUARTER, :],
                                         columns(t)[:, q * QUARTER:(q + 1) * QUARTER, :], ACT.Copy)\
                      .then_inc(l_high, 1)

            def norm(t, parity):
                act.wait_ge(peak_step, 6)
                act.wait_ge(quarter_used, 4 * t + 4)
                for half in range(2):
                    nc.scalar.activation(conv[:, half * HALF:(half + 1) * HALF], product[2 * parity + half][:, :],
                                         ACT.Relu, scale=unscale[:, :]).then_inc(relu_out, 1)
                for half in range(2):
                    root(2 * t + half, half * HALF_B, HALF_B)

            def root(count, b0, nb):
                act.wait_ge(var_ready, count + 1)
                nc.scalar.activation(std[:, b0:b0 + nb], squares[:, b0:b0 + nb], ACT.Sqrt, scale=1.0 / F,
                                     bias=epsc[:, :])\
                  .then_inc(std_ready, 1)

            l_highs(0, first=True)
            highs_to(HALVES)
            l_highs(1)
            norm(0, 0)
            with act.Fori(1, TILES - 2, 2) as t:
                l_highs(t + 1)
                act.wait_ge(out_ready, 2 * t)
                norm(t, 1)
                l_highs(t + 2)
                act.wait_ge(out_ready, 2 * t + 2)
                norm(t + 1, 0)
            act.wait_ge(out_ready, 2 * (TILES - 1))
            for piece, (b0, nb) in enumerate(LAST_PIECES):
                act.wait_ge(piece_done, piece + 1)
                nc.scalar.activation(conv[:, b0 * F:(b0 + nb) * F], last_product(piece), ACT.Relu,
                                     scale=unscale[:, :]).then_inc(relu_out, 1)
                root(2 * (TILES - 1) + piece, b0, nb)

        @block.vector
        def _(dve):
            def take_peak(k):
                dve.wait_ge(hw_kept, k + 1)
                nc.vector.tensor_reduce(peak[:, k:k + 1], H[:, k + AHEAD, :], AX.X, ALU.max,
                                        apply_absolute_value=True).then_inc(peak_kept, 1)

            def peak_over_tiles():
                dve.wait_ge(peak_kept, HALVES)
                nc.vector.tensor_reduce(peak1[:, :], peak[:, :], AX.X, ALU.max).then_inc(peak_step, 1)

            def peak_over_partitions():
                dve.wait_ge(peak_turned, 1)
                nc.vector.tensor_reduce(peakall[:, :], misc[0:1, 0:P], AX.X, ALU.max).then_inc(peak_step, 1)

            def scales():
                dve.wait_ge(peak_spread, 1)
                nc.vector.tensor_scalar(power[:, :], misc[:, P:P + 1], 2.0 ** -100, 2.0 ** 126, ALU.max, ALU.min)\
                  .then_inc(peak_step, 1)
                dve.wait_ge(peak_step, 3)
                nc.vector.tensor_scalar(power[:, :].bitcast(i32), power[:, :].bitcast(i32), 0x7F800000, None,
                                        ALU.bitwise_and).then_inc(peak_step, 1)
                dve.wait_ge(peak_step, 4)
                nc.vector.tensor_scalar(inverse[:, :].bitcast(i32), power[:, :].bitcast(i32), -1.0,
                                        float(254 << 23), ALU.mult, ALU.add).then_inc(peak_step, 1)
                nc.vector.tensor_scalar(unscale[:, :], power[:, :], 1.0 / (HW_TOP * L_SCALE), None, ALU.mult)\
                  .then_inc(peak_step, 1)
                dve.wait_ge(peak_step, 6)
                nc.vector.tensor_scalar(hw_scale[:, :], inverse[:, :], HW_TOP, None, ALU.mult).then_inc(scale_ready, 1)

            def low(k):
                dve.wait_ge(hw_high, k + 1)
                nc.vector.scalar_tensor_tensor(out=Hs[:, k, HALF:2 * HALF], in0=H[:, k + AHEAD, :],
                                               scalar=hw_scale[:, :], in1=Hs[:, k, 0:HALF],
                                               op0=ALU.mult, op1=ALU.subtract).then_inc(hw_low, 1)

            def add(n, k):
                i, j0, nb = GROUPS[k]
                area = S[:, i, j0 * P:(j0 + nb) * P]
                dve.wait_ge(adj_loaded[i][j0 // (TILES // 2)], 16)
                dve.wait_ge(adj_turned, k + 1)
                nc.vector.tensor_tensor(area, area, turned_of(n)[:, 0:nb * P], ALU.add).then_inc(sums_done, 1)

            def mirror(n, k):
                i, j0, nb = GROUPS[k]
                m, nb = MIRRORED.index(k), off_diagonal(k)
                dve.wait_ge(s_turned, m + 1)
                nc.vector.tensor_copy(S[:, j0:j0 + nb, i * P:(i + 1) * P],
                                      second_of(n)[:, 0:nb * P].rearrange("p (t n) -> p t n", n=P))\
                  .then_inc(mirrored_dve, 1)

            nc.vector.memset(lastsum, 0.0).then_inc(sums_cleared, 1)
            for n in range(len(STEPS) + LAG + 1):
                if n == X_END:
                    peak_over_tiles()
                if n == X_END + BEHIND + 1:
                    peak_over_partitions()
                if n == SCALES_STEP:
                    scales()
                if n - LAG - 1 in SECONDS:
                    kind, k = STEPS[n - LAG - 1]
                    if kind == "adj" and mirror_by_dve(k):
                        mirror(n - LAG - 1, k)
                if n < len(STEPS) and STEPS[n][0] == "adj":
                    add(n, STEPS[n][1])
                if n >= LAG + 2 and n - LAG - 2 < len(STEPS) and STEPS[n - LAG - 2][0] == "x":
                    take_peak(STEPS[n - LAG - 2][1])
                if n == LAST_QUARTER_STEP + LAG + 8:
                    dve.wait_ge(above_summed, 1 + sum(k < FIRST_OF_LAST for k in POOL_SUMS))
                    nc.vector.tensor_reduce(dhigh[:, 0:UPPER], above[:, 0:UPPER, :], AX.X, ALU.add)\
                      .then_inc(deg_step, 1)
                if n == SUMS_STEP + LAG + 3:
                    dve.wait_ge(above_summed, 1 + len(POOL_SUMS))
                    nc.vector.tensor_reduce(dhigh[:, UPPER:TILES], above[:, UPPER:TILES, :], AX.X, ALU.add)\
                      .then_inc(deg_step, 1)

            dve.wait_ge(relu_done, len(GROUPS))
            nc.vector.tensor_reduce(dlow[:, :], rowpart[:, :, :], AX.X, ALU.add).then_inc(deg_step, 1)
            dve.wait_ge(deg_step, 3)
            nc.vector.tensor_tensor(dlow[:, :], dlow[:, :], dhigh[:, :], ALU.add).then_inc(deg_step, 1)
            dve.wait_ge(last_summed, len(PE_SUMS))
            nc.vector.tensor_reduce(dlast[:, :], lastsum, AX.X, ALU.add).then_inc(deg_step, 1)
            dve.wait_ge(deg_step, 5)
            nc.vector.tensor_tensor(deg[:, :], dlow[:, :], dlast[:, :], ALU.add).then_inc(deg_step, 1)
            dve.wait_ge(deg_step, 6)
            nc.vector.scalar_tensor_tensor(out=degs[:, :], in0=deg[:, :], scalar=0.0, in1=deg[:, :],
                                           op0=ALU.is_le, op1=ALU.add).then_inc(deg_ready, 1)
            nc.vector.tensor_scalar(dmask[:, :], deg[:, :], 0.0, None, ALU.is_gt).then_inc(deg_step, 1)
            dve.wait_ge(root_done, 1)
            nc.vector.reciprocal(dinv[:, :], droot[:, :]).then_inc(deg_step, 1)
            dve.wait_ge(deg_step, 8)
            nc.vector.tensor_tensor(dtmp[:, :], dinv[:, :], dinv[:, :], ALU.mult).then_inc(deg_step, 1)
            nc.vector.tensor_tensor(dmask[:, :], dinv[:, :], dmask[:, :], ALU.mult).then_inc(deg_step, 1)
            dve.wait_ge(deg_step, 9)
            nc.vector.scalar_tensor_tensor(out=dtmp[:, :], in0=dtmp[:, :], scalar=-0.5, in1=degs[:, :],
                                           op0=ALU.mult, op1=ALU.mult).then_inc(deg_step, 1)
            dve.wait_ge(deg_step, 11)
            nc.vector.scalar_tensor_tensor(out=dinv[:, :], in0=dtmp[:, :], scalar=1.5, in1=dmask[:, :],
                                           op0=ALU.add, op1=ALU.mult).then_inc(d_ready, 1)
            dve.wait_ge(d_ready, 1)

            def l_left(t, rows):
                part = columns(t)[:, rows, :]
                nc.vector.tensor_tensor(part, part,
                                        dinv[:, rows].unsqueeze(2).to_broadcast([P, part.shape[1], P]), ALU.mult)\
                  .then_inc(l_step, 1)

            def l_right(t, parity, rows):
                part = columns(t)[:, rows, :]
                return nc.vector.tensor_tensor(part, part, drow(t, parity).to_broadcast([P, part.shape[1], P]),
                                               ALU.mult)

            def l_diagonal(t):
                block_tt = S[:, bass.ds(t, 1), bass.ds(t * P, P)].rearrange("p o n -> p (o n)")
                return nc.vector.tensor_tensor(block_tt, block_tt, minus[:, :], ALU.subtract)

            def l_tile(t, parity):
                rows = slice(0, TILES)
                l_left(t, rows)
                dve.wait_ge(l_step, 2 * t + 10)
                l_right(t, parity, rows).then_inc(l_step, 1)
                dve.wait_ge(l_step, 2 * t + 11)
                l_diagonal(t).then_inc(l_ready, 1)

            def l_low_quarter(t, q):
                dve.wait_ge(l_high, 4 * t + q + 1)
                part = slice(q * QUARTER, (q + 1) * QUARTER)
                nc.vector.tensor_tensor(Ll[:, part, :], columns(t)[:, part, :], Lh[:, part, :], ALU.subtract)\
                  .then_inc(l_low, 1)

            def l_lows(t):
                for q in range(4):
                    l_low_quarter(t, q)

            N_STEPS = 11

            def norm(t, parity, piece, b0, nb):
                part = slice(b0, b0 + nb)
                count = 2 * t + piece
                rows = conv[:, b0 * F:(b0 + nb) * F].rearrange("p (b f) -> p b f", f=F)
                if piece == 0:
                    dve.wait_ge(res_loaded[parity], 16 * ((t - parity) // 2 + 1))
                dve.wait_ge(relu_out, count + 1)
                nc.vector.tensor_tensor(rows, rows, columns(t)[:, part, :], ALU.add).then_inc(res_added, 1)
                dve.wait_ge(res_added, count + 1)
                for b in range(nb):
                    last = nc.vector.bn_stats(stats[:, b0 + b, :], rows[:, b, :])
                last.then_inc(n_step, 1)
                dve.wait_ge(n_step, count * N_STEPS + 1)
                m0, s0, m1, s1 = (stats[:, part, c] for c in (1, 2, 4, 5))
                nc.vector.tensor_tensor(apart[:, part], m0, m1, ALU.subtract).then_inc(n_step, 1)
                nc.vector.tensor_tensor(squares[:, part], s0, s1, ALU.add).then_inc(n_step, 1)
                nc.vector.tensor_tensor(mean[:, part], m0, m1, ALU.add).then_inc(n_step, 1)
                dve.wait_ge(n_step, count * N_STEPS + 4)
                nc.vector.scalar_tensor_tensor(out=apart[:, part], in0=apart[:, part], scalar=F / 4, in1=apart[:, part],
                                               op0=ALU.mult, op1=ALU.mult).then_inc(n_step, 1)
                nc.vector.tensor_scalar(mean[:, part], mean[:, part], 0.5, None, ALU.mult).then_inc(n_step, 1)
                dve.wait_ge(n_step, count * N_STEPS + 6)
                nc.vector.tensor_tensor(squares[:, part], squares[:, part], apart[:, part], ALU.add)\
                  .then_inc(var_ready, 1)
                dve.wait_ge(var_ready, count + 1)
                nc.vector.tensor_scalar(var[:, part], squares[:, part], 1.0 / F, EPS, ALU.mult, ALU.add)\
                  .then_inc(n_step, 1)
                dve.wait_ge(std_ready, count + 1)
                nc.vector.reciprocal(rstd[:, part], std[:, part]).then_inc(n_step, 1)
                dve.wait_ge(n_step, count * N_STEPS + 8)
                nc.vector.tensor_tensor(ntmp[:, part], rstd[:, part], rstd[:, part], ALU.mult).then_inc(n_step, 1)
                dve.wait_ge(n_step, count * N_STEPS + 9)
                nc.vector.scalar_tensor_tensor(out=ntmp[:, part], in0=ntmp[:, part], scalar=-0.5, in1=var[:, part],
                                               op0=ALU.mult, op1=ALU.mult).then_inc(n_step, 1)
                dve.wait_ge(n_step, count * N_STEPS + 10)
                nc.vector.scalar_tensor_tensor(out=rstd[:, part], in0=ntmp[:, part], scalar=1.5, in1=rstd[:, part],
                                               op0=ALU.add, op1=ALU.mult).then_inc(n_step, 1)
                dve.wait_ge(n_step, count * N_STEPS + 11)
                for b in range(nb):
                    at = b0 + b
                    last = nc.vector.tensor_scalar(columns(t)[:, B + at, :], rows[:, b, :], mean[:, at:at + 1],
                                                   rstd[:, at:at + 1], ALU.subtract, ALU.mult)
                last.then_inc(out_ready, 1)

            def lows_to(k):
                for m in range(lows_to.done, k):
                    if not by_pool(m):
                        low(m)
                lows_to.done = max(lows_to.done, k)

            lows_to.done = 0
            quarters = [slice(q * QUARTER, (q + 1) * QUARTER) for q in range(4)]
            l_left(0, quarters[0])
            l_left(0, quarters[1])
            dve.wait_ge(drow_ready, 1)
            dve.wait_ge(l_step, 1)
            l_right(0, 0, quarters[0]).then_inc(l_step, 1)
            dve.wait_ge(l_step, 3)
            l_diagonal(0).then_inc(l_ready, 1)
            l_right(0, 0, quarters[1]).then_inc(l_ready, 1)
            l_low_quarter(0, 0)
            lows_to(SPLIT_BEFORE_L)
            l_left(0, quarters[2])
            l_left(0, quarters[3])
            l_low_quarter(0, 1)
            lows_to(SPLIT_IN_L)
            dve.wait_ge(l_step, 5)
            l_right(0, 0, quarters[2]).then_inc(l_ready, 1)
            l_right(0, 0, quarters[3]).then_inc(l_ready, 1)
            l_low_quarter(0, 2)
            l_low_quarter(0, 3)
            for k in range(lows_to.done, HALVES):
                lows_to(k + 1)
                if 0 <= k - L1_FROM < 4:
                    l_left(1, quarters[k - L1_FROM])
                elif 4 <= k - L1_FROM < 8:
                    dve.wait_ge(drow_ready, 2)
                    dve.wait_ge(l_step, 9)
                    l_right(1, 1, quarters[k - L1_FROM - 4]).then_inc(l_step, 1)
                elif k - L1_FROM == 8:
                    dve.wait_ge(l_step, 13)
                    l_diagonal(1).then_inc(l_ready, 1)
            l_lows(1)
            for half in range(2):
                norm(0, 0, half, half * HALF_B, HALF_B)
            dve.wait_ge(drow_ready, TILES)
            with dve.Fori(2, TILES - 1, 2) as t:
                for parity in range(2):
                    l_tile(t + parity, parity)
                    l_lows(t + parity)
                    for half in range(2):
                        norm(t + parity - 1, 1 - parity, half, half * HALF_B, HALF_B)
            for piece, (b0, nb) in enumerate(LAST_PIECES):
                norm(TILES - 1, 1, piece, b0, nb)


def kernel(x, adj, L0_gnn_W):
    import numpy as np
    import concourse.bacc as bacc
    from concourse.bass_utils import run_bass_kernel_spmd

    nc = bacc.Bacc("TRN2", target_bir_lowering=False, num_devices=1, dynamic_dma_scratch_size=1024)
    arrays, args = {}, []
    for name, a in (("x", x), ("adj", adj), ("L0_gnn_W", L0_gnn_W)):
        a = np.ascontiguousarray(a)
        arrays[f"in_{name}"] = a
        args.append(nc.dram_tensor(f"in_{name}", a.shape, mybir.dt.from_np(a.dtype), kind="ExternalInput").ap())
    args.append(nc.dram_tensor("out", (B, N, F), mybir.dt.float32, kind="ExternalOutput").ap())
    gcn_layernorm(nc, *args)
    return run_bass_kernel_spmd(nc, [arrays], core_ids=[0]).results[0]["out"]
```
